# Optimizing a Trainium2 kernel written in Bass

```python
import numpy as np
import jax
import jax.numpy as jnp

def _softmax(x, axis=-1):
    return jax.nn.softmax(x, axis=axis)

def _gelu(x):
    return jax.nn.gelu(x, approximate=True)

def _silu(x):
    return jax.nn.silu(x)

def _sigmoid(x):
    return jax.nn.sigmoid(x)

def _layernorm(x, axis=-1, eps=1e-05):
    m = jnp.mean(x, axis=axis, keepdims=True)
    v = jnp.var(x, axis=axis, keepdims=True)
    return (x - m) / jnp.sqrt(v + eps)

def _scatter_add(tgt, idx, src, axis=0):
    return tgt.at[idx].add(src)

def _segment_sum(src, seg, n):
    return jax.ops.segment_sum(src, seg, n)
kernel_name = 'mk_hybrid_d1_jaxref_r8_55a07f'

def setup_inputs(seed: int=0):
    np.random.seed(seed)
    _w = jnp.asarray

    def _L0_attn_a_setup():
        import jax, jax.numpy as jnp
        import numpy as np
        B, T, C = (4, 512, 128)
        LN_EPS = 1e-05

        def _ln(x, g, b):
            m = x.mean(-1, keepdims=True)
            v = ((x - m) ** 2).mean(-1, keepdims=True)
            return (x - m) / jnp.sqrt(v + LN_EPS) * g + b

        def _shift(x, time_shift):
            b = x.shape[0]
            return jnp.concatenate([jnp.broadcast_to(time_shift, (b, 1, x.shape[2])), x[:, :-1]], axis=1)

        def _wkv(w, u, k, v):
            b, t, c = k.shape
            aa0 = jnp.zeros((b, c), k.dtype)
            bb0 = jnp.ones((b, c), k.dtype)
            pp0 = jnp.full((b, c), -1e+38, k.dtype)

            def step(carry, kv_t):
                aa, bb, pp = carry
                kk, vv = kv_t
                uu_kk = u + kk
                p = jnp.maximum(pp, uu_kk)
                e1 = jnp.exp(pp - p)
                e2 = jnp.exp(uu_kk - p)
                y = (e1 * aa + e2 * vv) / (e1 * bb + e2)
                ww_kk = w + kk
                pu = jnp.maximum(pp + w, ww_kk)
                e1u = jnp.exp(pp + w - pu)
                e2u = jnp.exp(ww_kk - pu)
                aa_n = e1u * aa + e2u * vv
                bb_n = e1u * bb + e2u
                pp_n = pu + jnp.log(bb_n)
                return ((aa_n, bb_n, pp_n), y)
            _, ys = jax.lax.scan(step, (aa0, bb0, pp0), (k.transpose(1, 0, 2), v.transpose(1, 0, 2)))
            return ys.transpose(1, 0, 2)
        key = jax.random.key(seed)
        ks = jax.random.split(key, 10)
        s1 = 1.0 / np.sqrt(C)
        s4 = 1.0 / np.sqrt(4 * C)
        return {'x': jax.random.normal(ks[0], (B, T, C), jnp.float32), 'time_decay': jax.random.normal(ks[1], (C,), jnp.float32), 'time_first': jax.random.normal(ks[2], (C,), jnp.float32), 'time_shift': jnp.zeros((1, 1, C), jnp.float32), 'Wk': jax.random.normal(ks[3], (C, C), jnp.float32) * s1, 'Wv': jax.random.normal(ks[4], (C, C), jnp.float32) * s1, 'Wr': jax.random.normal(ks[5], (C, C), jnp.float32) * s1, 'Wck': jax.random.normal(ks[6], (C, 4 * C), jnp.float32) * s1, 'Wcv': jax.random.normal(ks[7], (4 * C, C), jnp.float32) * s4, 'Wcr': jax.random.normal(ks[8], (C, C), jnp.float32) * s1, 'ln1_g': jnp.ones((C,), jnp.float32), 'ln1_b': jnp.zeros((C,), jnp.float32), 'ln2_g': jnp.ones((C,), jnp.float32), 'ln2_b': jnp.zeros((C,), jnp.float32)}
    _L0_attn_a_in = _L0_attn_a_setup()

    def _L0_attn_b_setup():
        import math
        import jax, jax.numpy as jnp
        import numpy as np
        D_MODEL = 128
        NUM_SCALES = 4
        STATE_SIZE = 16
        EXPAND = 2
        D_INNER = D_MODEL * EXPAND
        D_PER_SCALE = D_INNER // NUM_SCALES
        BATCH, SEQ = (4, 512)

        def _make_A_log():
            base = np.arange(1, STATE_SIZE + 1, dtype=np.float32)
            parts = [np.broadcast_to(base * 2.0 ** i, (D_PER_SCALE, STATE_SIZE)) for i in range(NUM_SCALES)]
            A = np.concatenate(parts, axis=0)
            return jnp.asarray(np.log(A))

        def _selective_scan(x_ssm, A, B_mat, C_mat, dt):
            b, L, d = x_ssm.shape
            N = A.shape[1]
            h0 = jnp.zeros((b, d, N), dtype=jnp.float32)

            def step(h, inp):
                dt_t, B_t, C_t, x_t = inp
                A_bar = jnp.exp(jnp.minimum(dt_t[..., None] * A, 20.0))
                B_bar = dt_t[..., None] * B_t[:, None, :]
                h = A_bar * h + B_bar * x_t[..., None]
                y_t = jnp.einsum('bdn,bn->bd', h, C_t)
                return (h, y_t)
            xs = (jnp.swapaxes(dt, 0, 1), jnp.swapaxes(B_mat, 0, 1), jnp.swapaxes(C_mat, 0, 1), jnp.swapaxes(x_ssm, 0, 1))
            _, ys = jax.lax.scan(step, h0, xs)
            return jnp.swapaxes(ys, 0, 1)
        key = jax.random.key(seed)
        ks = jax.random.split(key, 8)
        scale = 0.02
        x = jax.random.normal(ks[0], (BATCH, SEQ, D_MODEL), dtype=jnp.float32)
        W_in = jax.random.normal(ks[1], (2 * D_INNER, D_MODEL), dtype=jnp.float32) * scale
        W_B = jax.random.normal(ks[2], (STATE_SIZE, D_INNER), dtype=jnp.float32) * scale
        W_C = jax.random.normal(ks[3], (STATE_SIZE, D_INNER), dtype=jnp.float32) * scale
        W_dt = jax.random.normal(ks[4], (D_INNER, D_INNER), dtype=jnp.float32) * scale
        u = jax.random.uniform(ks[5], (D_INNER,), dtype=jnp.float32)
        b_dt = u * (math.log(0.1) - math.log(0.001)) + math.log(0.001)
        W_out = jax.random.normal(ks[6], (D_MODEL, D_INNER), dtype=jnp.float32) * scale
        A_log = _make_A_log()
        D = jnp.ones((D_INNER,), dtype=jnp.float32)
        output_gate = jnp.zeros((1,), dtype=jnp.float32)
        return {'x': x, 'W_in': W_in, 'A_log': A_log, 'W_B': W_B, 'W_C': W_C, 'W_dt': W_dt, 'b_dt': b_dt, 'D': D, 'output_gate': output_gate, 'W_out': W_out}
    _L0_attn_b_in = _L0_attn_b_setup()

    def _L0_ffn_setup():
        import jax, jax.numpy as jnp
        import numpy as np
        EMB, HID, E, TOPK = (128, 512, 8, 2)
        key = jax.random.key(seed)
        ks = jax.random.split(key, 10)
        s = 0.02
        return {'x': jax.random.normal(ks[0], (4, 256, EMB), jnp.float32), 'rw1': s * jax.random.normal(ks[1], (EMB, HID), jnp.float32), 'rb1': jnp.zeros((HID,), jnp.float32), 'rw2': s * jax.random.normal(ks[2], (HID, E), jnp.float32), 'rb2': jnp.zeros((E,), jnp.float32), 'w1': s * jax.random.normal(ks[3], (E, EMB, HID), jnp.float32), 'b1': jnp.zeros((E, HID), jnp.float32), 'w2': s * jax.random.normal(ks[4], (E, HID, EMB), jnp.float32), 'b2': jnp.zeros((E, EMB), jnp.float32)}
    _L0_ffn_in = _L0_ffn_setup()
    _d = {'L0_attn_a_x': _L0_attn_a_in['x'], 'L0_attn_a_time_decay': _L0_attn_a_in['time_decay'], 'L0_attn_a_time_first': _L0_attn_a_in['time_first'], 'L0_attn_a_time_shift': _L0_attn_a_in['time_shift'], 'L0_attn_a_Wk': _L0_attn_a_in['Wk'], 'L0_attn_a_Wv': _L0_attn_a_in['Wv'], 'L0_attn_a_Wr': _L0_attn_a_in['Wr'], 'L0_attn_a_Wck': _L0_attn_a_in['Wck'], 'L0_attn_a_Wcv': _L0_attn_a_in['Wcv'], 'L0_attn_a_Wcr': _L0_attn_a_in['Wcr'], 'L0_attn_a_ln1_g': _L0_attn_a_in['ln1_g'], 'L0_attn_a_ln1_b': _L0_attn_a_in['ln1_b'], 'L0_attn_a_ln2_g': _L0_attn_a_in['ln2_g'], 'L0_attn_a_ln2_b': _L0_attn_a_in['ln2_b'], 'L0_attn_b_W_in': _L0_attn_b_in['W_in'], 'L0_attn_b_A_log': _L0_attn_b_in['A_log'], 'L0_attn_b_W_B': _L0_attn_b_in['W_B'], 'L0_attn_b_W_C': _L0_attn_b_in['W_C'], 'L0_attn_b_W_dt': _L0_attn_b_in['W_dt'], 'L0_attn_b_b_dt': _L0_attn_b_in['b_dt'], 'L0_attn_b_D': _L0_attn_b_in['D'], 'L0_attn_b_output_gate': _L0_attn_b_in['output_gate'], 'L0_attn_b_W_out': _L0_attn_b_in['W_out'], 'L0_ffn_rw1': _L0_ffn_in['rw1'], 'L0_ffn_rb1': _L0_ffn_in['rb1'], 'L0_ffn_rw2': _L0_ffn_in['rw2'], 'L0_ffn_rb2': _L0_ffn_in['rb2'], 'L0_ffn_w1': _L0_ffn_in['w1'], 'L0_ffn_b1': _L0_ffn_in['b1'], 'L0_ffn_w2': _L0_ffn_in['w2'], 'L0_ffn_b2': _L0_ffn_in['b2']}
    _x0 = _d['L0_attn_a_x']
    _d['L0_attn_a_x'] = jax.random.normal(jax.random.fold_in(jax.random.key(seed), 1), (4, 1024, 128), dtype=_x0.dtype)
    del _x0
    return _d

def reference(L0_attn_a_x, L0_attn_a_time_decay, L0_attn_a_time_first, L0_attn_a_time_shift, L0_attn_a_Wk, L0_attn_a_Wv, L0_attn_a_Wr, L0_attn_a_Wck, L0_attn_a_Wcv, L0_attn_a_Wcr, L0_attn_a_ln1_g, L0_attn_a_ln1_b, L0_attn_a_ln2_g, L0_attn_a_ln2_b, L0_attn_b_W_in, L0_attn_b_A_log, L0_attn_b_W_B, L0_attn_b_W_C, L0_attn_b_W_dt, L0_attn_b_b_dt, L0_attn_b_D, L0_attn_b_output_gate, L0_attn_b_W_out, L0_ffn_rw1, L0_ffn_rb1, L0_ffn_rw2, L0_ffn_rb2, L0_ffn_w1, L0_ffn_b1, L0_ffn_w2, L0_ffn_b2):

    def _L0_attn_a_ref(x, time_decay, time_first, time_shift, Wk, Wv, Wr, Wck, Wcv, Wcr, ln1_g, ln1_b, ln2_g, ln2_b):
        import jax, jax.numpy as jnp
        import numpy as np
        B, T, C = (4, 512, 128)
        LN_EPS = 1e-05

        def _ln(x, g, b):
            m = x.mean(-1, keepdims=True)
            v = ((x - m) ** 2).mean(-1, keepdims=True)
            return (x - m) / jnp.sqrt(v + LN_EPS) * g + b

        def _shift(x, time_shift):
            b = x.shape[0]
            return jnp.concatenate([jnp.broadcast_to(time_shift, (b, 1, x.shape[2])), x[:, :-1]], axis=1)

        def _wkv(w, u, k, v):
            b, t, c = k.shape
            aa0 = jnp.zeros((b, c), k.dtype)
            bb0 = jnp.ones((b, c), k.dtype)
            pp0 = jnp.full((b, c), -1e+38, k.dtype)

            def step(carry, kv_t):
                aa, bb, pp = carry
                kk, vv = kv_t
                uu_kk = u + kk
                p = jnp.maximum(pp, uu_kk)
                e1 = jnp.exp(pp - p)
                e2 = jnp.exp(uu_kk - p)
                y = (e1 * aa + e2 * vv) / (e1 * bb + e2)
                ww_kk = w + kk
                pu = jnp.maximum(pp + w, ww_kk)
                e1u = jnp.exp(pp + w - pu)
                e2u = jnp.exp(ww_kk - pu)
                aa_n = e1u * aa + e2u * vv
                bb_n = e1u * bb + e2u
                pp_n = pu + jnp.log(bb_n)
                return ((aa_n, bb_n, pp_n), y)
            _, ys = jax.lax.scan(step, (aa0, bb0, pp0), (k.transpose(1, 0, 2), v.transpose(1, 0, 2)))
            return ys.transpose(1, 0, 2)
        h = _ln(x, ln1_g, ln1_b)
        hs = _shift(h, time_shift)
        k = hs @ Wk
        v = hs @ Wv
        r = hs @ Wr
        y = _wkv(time_decay, time_first, k, v)
        x = x + jax.nn.sigmoid(r) * y
        h2 = _ln(x, ln2_g, ln2_b)
        h2s = _shift(h2, time_shift)
        kk = jnp.square(jax.nn.relu(h2s @ Wck))
        kv = kk @ Wcv
        rr = jax.nn.sigmoid(h2s @ Wcr)
        x = x + rr * kv
        return x

    def _L0_attn_b_ref(x, W_in, A_log, W_B, W_C, W_dt, b_dt, D, output_gate, W_out):
        import math
        import jax, jax.numpy as jnp
        import numpy as np
        D_MODEL = 128
        NUM_SCALES = 4
        STATE_SIZE = 16
        EXPAND = 2
        D_INNER = D_MODEL * EXPAND
        D_PER_SCALE = D_INNER // NUM_SCALES
        BATCH, SEQ = (4, 512)

        def _make_A_log():
            base = np.arange(1, STATE_SIZE + 1, dtype=np.float32)
            parts = [np.broadcast_to(base * 2.0 ** i, (D_PER_SCALE, STATE_SIZE)) for i in range(NUM_SCALES)]
            A = np.concatenate(parts, axis=0)
            return jnp.asarray(np.log(A))

        def _selective_scan(x_ssm, A, B_mat, C_mat, dt):
            b, L, d = x_ssm.shape
            N = A.shape[1]
            h0 = jnp.zeros((b, d, N), dtype=jnp.float32)

            def step(h, inp):
                dt_t, B_t, C_t, x_t = inp
                A_bar = jnp.exp(jnp.minimum(dt_t[..., None] * A, 20.0))
                B_bar = dt_t[..., None] * B_t[:, None, :]
                h = A_bar * h + B_bar * x_t[..., None]
                y_t = jnp.einsum('bdn,bn->bd', h, C_t)
                return (h, y_t)
            xs = (jnp.swapaxes(dt, 0, 1), jnp.swapaxes(B_mat, 0, 1), jnp.swapaxes(C_mat, 0, 1), jnp.swapaxes(x_ssm, 0, 1))
            _, ys = jax.lax.scan(step, h0, xs)
            return jnp.swapaxes(ys, 0, 1)
        xz = jnp.einsum('bld,ed->ble', x, W_in)
        x_ssm, z = jnp.split(xz, 2, axis=-1)
        A = -jnp.exp(A_log.astype(jnp.float32))
        B_mat = jnp.einsum('bld,nd->bln', x_ssm, W_B)
        C_mat = jnp.einsum('bld,nd->bln', x_ssm, W_C)
        dt = jax.nn.softplus(jnp.einsum('bld,ed->ble', x_ssm, W_dt) + b_dt)
        y = _selective_scan(x_ssm.astype(jnp.float32), A, B_mat.astype(jnp.float32), C_mat.astype(jnp.float32), dt.astype(jnp.float32))
        y = y + x_ssm * D[None, None, :]
        y = y * jax.nn.silu(z)
        out = jnp.einsum('ble,de->bld', y, W_out) * jax.nn.sigmoid(output_gate)
        return out

    def _L0_ffn_ref(x, rw1, rb1, rw2, rb2, w1, b1, w2, b2):
        import jax, jax.numpy as jnp
        import numpy as np
        EMB, HID, E, TOPK = (128, 512, 8, 2)
        B, S, D = x.shape
        logits = jax.nn.silu(jnp.einsum('bsd,dh->bsh', x, rw1) + rb1)
        logits = jnp.einsum('bsh,he->bse', logits, rw2) + rb2
        k_logits, k_index = jax.lax.top_k(logits, TOPK)
        k_prob = jax.nn.softmax(k_logits, axis=-1)
        xf = x.reshape(B * S, D)
        k_index_f = k_index.reshape(B * S, TOPK)
        k_prob_f = k_prob.reshape(B * S, TOPK)
        out = jnp.zeros_like(xf)
        for e in range(E):
            we = jnp.sum(jnp.where(k_index_f == e, k_prob_f, 0.0), axis=-1)
            h = jax.nn.silu(xf @ w1[e] + b1[e]) @ w2[e] + b2[e]
            out = out + we[:, None] * h
        return out.reshape(B, S, D)
    x = L0_attn_a_x
    x = x + _L0_attn_a_ref(_layernorm(x, axis=-1), L0_attn_a_time_decay, L0_attn_a_time_first, L0_attn_a_time_shift, L0_attn_a_Wk, L0_attn_a_Wv, L0_attn_a_Wr, L0_attn_a_Wck, L0_attn_a_Wcv, L0_attn_a_Wcr, L0_attn_a_ln1_g, L0_attn_a_ln1_b, L0_attn_a_ln2_g, L0_attn_a_ln2_b)
    x = x + _L0_ffn_ref(_layernorm(x, axis=-1), L0_ffn_rw1, L0_ffn_rb1, L0_ffn_rw2, L0_ffn_rb2, L0_ffn_w1, L0_ffn_b1, L0_ffn_w2, L0_ffn_b2)
    x = x + _L0_attn_b_ref(_layernorm(x, axis=-1), L0_attn_b_W_in, L0_attn_b_A_log, L0_attn_b_W_B, L0_attn_b_W_C, L0_attn_b_W_dt, L0_attn_b_b_dt, L0_attn_b_D, L0_attn_b_output_gate, L0_attn_b_W_out)
    x = x + _L0_ffn_ref(_layernorm(x, axis=-1), L0_ffn_rw1, L0_ffn_rb1, L0_ffn_rw2, L0_ffn_rb2, L0_ffn_w1, L0_ffn_b1, L0_ffn_w2, L0_ffn_b2)
    return x

_drawn_inputs = setup_inputs


def setup_inputs(seed=0):
    import zlib

    import numpy as np

    out = dict(_drawn_inputs(seed))
    spreads = {'L0_attn_a_time_shift': (0.0, 0.523),
     'L0_attn_a_ln1_g': (1.0, 0.2),
     'L0_attn_a_ln1_b': (0.0, 0.1),
     'L0_attn_a_ln2_g': (1.0, 0.2),
     'L0_attn_a_ln2_b': (0.0, 0.1),
     'L0_attn_b_D': (1.0, 0.6),
     'L0_ffn_rb1': (0.0, 0.296),
     'L0_ffn_rb2': (0.0, 0.1),
     'L0_ffn_b1': (0.0, 0.485),
     'L0_ffn_b2': (0.0, 0.1)}
    factors = {'L0_attn_b_W_in': 8.0,
     'L0_attn_b_A_log': 8.0,
     'L0_attn_b_W_B': 8.0,
     'L0_attn_b_W_C': 8.0,
     'L0_attn_b_W_dt': 8.0,
     'L0_attn_b_b_dt': 8.0,
     'L0_attn_b_W_out': 8.0}
    for name, (base, spread) in spreads.items():
        noise = np.random.default_rng([zlib.crc32(name.encode()), seed]).standard_normal(out[name].shape)
        drawn = base * np.exp(spread * noise) if base else spread * noise
        out[name] = jnp.asarray(drawn.astype(out[name].dtype))
    for name, factor in factors.items():
        out[name] = (out[name] * factor).astype(out[name].dtype)
    return out
```

```python
from contextlib import ExitStack

import concourse.bass as bass
from concourse import mybir

F32 = mybir.dt.float32
U32 = mybir.dt.uint32
I32 = mybir.dt.int32
ALU = mybir.AluOpType
ACT = mybir.ActivationFunctionType
AX = mybir.AxisListType

P = 128
B, T, C = 4, 1024, 128
TC = 128
NCH = T // TC
N = B * TC
E, HID, TOPK = 8, 512, 2
HB = HID // P
DI, NS = 256, 16
DH = DI // P
NG = 4
Q = NS // NG
UNITS = Q * DH
R_MAX = 2.0 ** 80
G_MIN, G_MAX = -80.0, 25.0
LN_FROM = 1.0 / 32
EPS = 1e-5
STAGES = 4
RWKV, FFN0, MAMBA, FFN1 = range(STAGES)
FFN = (FFN0, FFN1)
STATS = "natural_log_exp_and_others"
SILU = "silu_and_others"


def order(*names):
    return {name: k + 1 for k, name in enumerate(names)}


def at(chunk, steps, name):
    return chunk * len(steps) + steps[name]


def loads_by(chunk, per_chunk, k):
    return 16 * (chunk * per_chunk + k)


def rows_in(chunk, k):
    return loads_by(chunk, len(range(k % 3, 2 * Q, 3)), k // 3 + 1)


def build(nc, a, out):
    assert E == UNITS and TC % E == 0
    STEPS = TC // E

    R_PE = order("xT", "mean0", "var0", "mean1", "var1", "k", "v", "r", "mean2", "var2",
                 "ck0", "ck1", "ck2", "ck3", "kv", "cr")
    R_ACT = order("xin", "sq0", "ln0", "rstd0", "sq1", "ln1", "rstd1", "h", "k", "v", "gamma", "tr",
                  "sq2", "ln2", "rstd2", "h2", "relu0", "kk0", "relu1", "kk1", "relu2", "kk2",
                  "relu3", "kk3", "trc")
    R_DVE = order("h", "h2", "k", "aa", "p", "c", "xc0", "x0", "xc1", "xn1", "dk", "dkc",
                  "rmin", "vc", "aa0", "aa1", "aa2", "aa3", "ra", "den", "rden", "num", "y", "ys",
                  "x1", "xc2", "xn2", "s", "x2", "X")
    M_PE = order("mean", "var", "xs0", "xs1", "bc", "dt0", "dt1", "z0", "z1", "out")
    M_ACT = order("sq", "ln", "rstd", "xs0", "xs1", "bc", "ab0", "ab1", "ex0", "ex1", "lp0", "lp1",
                  "sz0", "sz1", *[f"exp{j}_{n}" for j in range(UNITS) for n in range(NG)])
    M_DVE = order("xc", "xn", "mx0", "mx1", "p00", "p01", "p10", "p11", "p20", "p21", "g0", "g1", "lc0", "lc1", "dt0", "dt1", "u0", "u1",
                  *[f"{s}{j}" for j in range(UNITS) for s in ("scan", "save", "red", "acc") if s != "acc" or j >= DH],
                  "y0", "y1", "yz0", "yz1", "X")
    M_POOL = order("bu0", "edge0", *[s for j in range(UNITS) for s in
                   ([f"bu{j + 1}", f"edge{j + 1}"] if j + 1 < UNITS else []) + [f"hc{j}"]])
    F_PE = order("mean", "var", "r0", "r1", "r2", "r3", "logits", "weT",
                 *[s for e in range(E) for s in [f"h{e}_{k}" for k in range(HB)] + [f"out{e}"]])
    F_PE = (F_PE, order(*F_PE, "oT"))
    F_ACT = order("sq", "ln", "rstd", "sr0", "sr1", "sr2", "sr3", "gex", "weT",
                  *[f"h{e}_{k}" for e in range(E) for k in range(HB)])
    F_ACT = (F_ACT, order(*F_ACT, "xo", "o"))
    F_DVE = order("xc", "xn", "idxf",
                  "d", "den", "p0", "p1", "m0", "w0", "m1", "w1", "we", *[f"t{e}" for e in range(E)])
    F_DVE = (F_DVE, F_DVE)
    F_POOL = order(*[f"acc{e}" for e in range(E)])
    F_POOL = (F_POOL, F_POOL)

    with ExitStack() as ctx:
        def sb(name, shape, dt=F32):
            return ctx.enter_context(nc.sbuf_tensor(name, shape, dt))

        def bank(name):
            return ctx.enter_context(nc.psum_tensor(name, [P, N], F32))

        def sem(name):
            return ctx.enter_context(nc.semaphore(name))

        ident = sb("ident", [P, P])
        ones_mean = sb("ones_mean", [P, P])
        eps = sb("eps", [P, 1])
        iota_i = sb("iota_i", [P, E], I32)
        iota_f = sb("iota_f", [P, E])
        Wk, Wv, Wr, Wcr = (sb(n, [P, C]) for n in ("Wk", "Wv", "Wr", "Wcr"))
        Wck = sb("Wck", [P, HID])
        Wcv = sb("Wcv", [P, HB, C])
        cols = sb("cols", [P, 8])
        W_COL, U_COL, TS_COL, G1, B1, G2, B2, EU = range(8)
        WinT = sb("WinT", [P, 2 * DI])
        WbcT = sb("WbcT", [P, DH, 2 * NS])
        WdtT = sb("WdtT", [P, DH, DI])
        WoutT = sb("WoutT", [P, DH, C])
        Aneg = sb("Aneg", [P, DH, NS])
        bdt = sb("bdt", [P, DH])
        Dp = sb("Dp", [P, DH])
        gate = sb("gate", [P, 1])
        rw1 = sb("rw1", [P, HID])
        rb1 = sb("rb1", [P, HB])
        rw2 = sb("rw2", [P, HB, E])
        rb2 = sb("rb2", [P, E])
        w1 = sb("w1", [P, E, HID])
        b1 = sb("b1", [P, E, HB])
        w2 = sb("w2", [P, E, HB, C])
        b2 = sb("b2", [P, E])

        X = sb("X", [P, NCH, N])

        xtok = sb("xtok", [P, B, C])
        xin = sb("xin", [P, N])
        x0 = sb("x0", [P, N])
        xc_r = sb("xc_r", [P, N])
        sq_r = sb("sq_r", [P, N])
        rs_r = sb("rs_r", [P, N])
        hs1 = sb("hs1", [P, B, TC + 1])
        hs2 = sb("hs2", [P, B, TC + 1])
        kb = sb("kb", [P, B, TC + 1])
        aab = sb("aab", [P, B, TC + 1])
        pb = sb("pb", [P, B, TC + 1])
        cb = sb("cb", [P, B, TC + 1])
        vb = sb("vb", [P, B, TC])
        gam = sb("gam", [P, B, TC])
        rb = sb("rb", [P, B, TC])
        bbs = sb("bbs", [P, 2, B])
        rcp = sb("rcp", [P, B])
        tr = xc_r

        rs_m = sb("rs_m", [P, N])
        xs = sb("xs", [P, DH, B, TC])
        sz = sb("sz", [P, DH, N])
        dt = sb("dt", [P, DH, N])
        du = sb("du", [P, DH, B, TC])
        ya = sb("ya", [P, DH, N])
        yr = sb("yr", [P, N])
        sq_m = ya[:, 0, :]
        xc_m = yr
        mx = sz
        bcs = yr[0:2 * NS, :]
        bcb = sb("bcb", [P, 3, NG, N])
        abuf = sb("abuf", [P, DH, NG, B, TC + 1])
        bbuf = sb("bbuf", [P, DH, NG, B, TC + 1])
        hst = sb("hst", [P, UNITS, NG, B])

        xf = [sb(f"xf{l}", [P, N]) for l in range(2)]
        t1 = [sb(f"t1_{l}", [P, N]) for l in range(2)]
        hid = [sb(f"hid{l}", [P, HB, N]) for l in range(2)]
        wb = [sb(f"wb{l}", [P, 2, N]) for l in range(2)]
        lg = [sb(f"lg{l}", [P, B, E]) for l in range(2)]
        top = [sb(f"top{l}", [P, B, E]) for l in range(2)]
        idx = [sb(f"idx{l}", [P, B, E], U32) for l in range(2)]
        idf = [sb(f"idf{l}", [P, B, E]) for l in range(2)]
        gp = [sb(f"gp{l}", [P, 5, B]) for l in range(2)]
        mk = [sb(f"mk{l}", [P, 2, B, E]) for l in range(2)]
        we = [mk[l][:, 0] for l in range(2)]
        weT = [t1[l][0:E, :] for l in range(2)]
        xo = xf[1]
        otok = xtok
        kk = hid[0]

        we_dram = [nc.dram_tensor(f"we_scratch{l}", [E, N], F32, kind="Internal").ap() for l in range(2)]
        bc_dram = nc.dram_tensor("bc_scratch", [2, NS, N], F32, kind="Internal").ap()

        A0, A1, M0, M1, H0, H1, O0, O1 = (bank(n) for n in ("A0", "A1", "M0", "M1", "H0", "H1", "O0", "O1"))
        OB = (O0, O1)
        HR = ((H0, H1), (M0, M1))

        s_load = sem("s_load")
        s_wtok = sem("s_wtok")
        s_setup_pool = sem("s_setup_pool")
        s_setup_pe = sem("s_setup_pe")
        s_setup_act = sem("s_setup_act")
        s_setup_dve = sem("s_setup_dve")
        pe_done, act_done, dve_done, pool_done = (sem(f"{n}_done") for n in ("pe", "act", "dve", "pool"))
        s_release = sem("s_release")
        r_pe, r_act, r_dve, s_wkv, s_x = (sem(n) for n in ("r_pe", "r_act", "r_dve", "s_wkv", "s_x"))
        s_adding = [sem(f"s_adding{l}") for l in range(2)]
        s_top = [sem(f"s_top{l}") for l in range(2)]
        m_pe, m_act, m_dve, m_pool = (sem(n) for n in ("m_pe", "m_act", "m_dve", "m_pool"))
        f_pe, f_act, f_dve, f_pool = ([sem(f"f{l}_{n}") for l in range(2)] for n in ("pe", "act", "dve", "pool"))
        s_bcw = sem("s_bcw")
        s_bcb = [sem(f"s_bcb{k}") for k in range(3)]
        s_wew = [sem(f"s_wew{l}") for l in range(2)]
        s_wb = [[sem(f"s_wb{l}_{k}") for k in range(2)] for l in range(2)]
        s_out = sem("s_out")
        block = ctx.enter_context(nc.Block())

        def pipeline(eng, iteration):
            last = NCH + STAGES - 1
            full = (STAGES - 1, NCH)
            for i in range(full[0]):
                iteration(i, [s for s in range(STAGES) if 0 <= i - s < NCH])
            with eng.Fori(*full) as i:
                iteration(i, list(range(STAGES)))
            for i in range(full[1], last):
                iteration(i, [s for s in range(STAGES) if 0 <= i - s < NCH])

        def meet(eng, done, i):
            eng.drain().then_inc(done, 1)
            eng.wait_ge(s_release, i + 1)

        def layers(on):
            return [(l, s) for l, s in enumerate(FFN) if s in on]

        loads = [
            (Wk[:], a["Wk"]), (Wv[:], a["Wv"]), (Wr[:], a["Wr"]), (Wcr[:], a["Wcr"]), (Wck[:], a["Wck"]),
            (Wcv[:], a["Wcv"].rearrange("(k p) c -> p k c", p=P)),
            *[(cols[:, k:k + 1], a[n]) for n, k in (("time_decay", W_COL), ("time_first", U_COL), ("ts", TS_COL),
              ("ln1_g", G1), ("ln1_b", B1), ("ln2_g", G2), ("ln2_b", B2))],
            (Aneg[:], a["A_log"].rearrange("(h p) n -> p h n", p=P)),
            (gate[:], a["output_gate"].partition_broadcast(P)),
            (rw1[:], a["rw1"]),
            (rw2[:], a["rw2"].rearrange("(k p) e -> p k e", p=P)),
            (rb2[:], a["rb2"].partition_broadcast(P)),
            (w1[:], a["w1"].rearrange("e c h -> c e h")),
            (w2[:], a["w2"].rearrange("e (k p) c -> p e k c", p=P)),
        ]
        element_loads = [
            (bdt[:], a["b_dt"].rearrange("(h p) -> p h", p=P)),
            (Dp[:], a["D"].rearrange("(h p) -> p h", p=P)),
            (rb1[:], a["rb1"].rearrange("(k p) -> p k", p=P)),
            *[(b1[:, e, :], a["b1"][e].rearrange("(k p) -> p k", p=P)) for e in range(E)],
            (b2[:], a["b2"].rearrange("e c -> c e")),
        ]
        win_tok = sz[:].rearrange("p h (k c) -> p (h k) c", c=C)[:, 0:4, :]
        wdt_tok = hid[0][:, 0:DH, 0:DI]
        wbc_tok = hid[1][0:2 * NS, 0, 0:DI]
        wout_tok = hid[1][:, 1, 0:DI]
        tok_loads = [
            (win_tok, a["W_in"].rearrange("(k p) c -> p k c", p=P)),
            (wdt_tok, a["W_dt"].rearrange("(h p) d -> p h d", p=P)),
            (wbc_tok[0:NS], a["W_B"]), (wbc_tok[NS:2 * NS], a["W_C"]),
            (wout_tok, a["W_out"]),
        ]
        n_load, n_tok = 16 * (len(loads) + len(element_loads)), 16 * len(tok_loads)

        @block.sync
        def _(sp):
            for dst, src in tok_loads:
                sp.dma_start(dst, src).then_inc(s_wtok, 16)
            for dst, src in loads:
                sp.dma_start(dst, src).then_inc(s_load, 16)
            for dst, src in element_loads:
                sp.dma_start(dst, src, allow_slow_non_contiguous=True).then_inc(s_load, 16)

            def iteration(i, on):
                c = {s: i - s for s in on}
                if RWKV in on:
                    sp.dma_start(xtok[:], a["x"][:, bass.ds(i, 1), :, :].rearrange("b o t c -> t (o b) c")
                                 ).then_inc(s_x, 16)

                def bc_rows(k):
                    q, part = divmod(k, 2)
                    sp.dma_start(bcb[:, k % 3], bc_dram[part, q * NG:(q + 1) * NG, :].partition_broadcast(P)
                                 ).then_inc(s_bcb[k % 3], 16)

                def we_row(l, e):
                    sp.dma_start(wb[l][:, e % 2, :], we_dram[l][e].partition_broadcast(P)
                                 ).then_inc(s_wb[l][e % 2], 16)

                if MAMBA in on:
                    sp.wait_ge(m_act, at(c[MAMBA], M_ACT, "bc"))
                    sp.dma_start(bc_dram.rearrange("k n t -> (k n) t"), bcs).then_inc(s_bcw, 16)
                    sp.wait_ge(s_bcw, loads_by(c[MAMBA], 1, 1))
                    for k in range(3):
                        bc_rows(k)
                for l, _ in layers(on):
                    sp.wait_ge(f_act[l], at(c[FFN[l]], F_ACT[l], "weT"))
                    sp.dma_start(we_dram[l], weT[l]).then_inc(s_wew[l], 16)
                for l, _ in layers(on):
                    sp.wait_ge(s_wew[l], loads_by(c[FFN[l]], 1, 1))
                    we_row(l, 0)
                    we_row(l, 1)
                for j in range(E):
                    if MAMBA in on and j % 2:
                        for k, used in ((j + 2, f"bu{j}"), (j + 3, f"hc{j}")):
                            if k < 2 * Q:
                                sp.wait_ge(m_pool, at(c[MAMBA], M_POOL, used))
                                bc_rows(k)
                    if j + 2 < E:
                        for l, _ in layers(on):
                            sp.wait_ge(f_dve[l], at(c[FFN[l]], F_DVE[l], f"t{j}"))
                            we_row(l, j + 2)
                if FFN1 in on:
                    sp.wait_ge(f_act[1], at(c[FFN1], F_ACT[1], "o"))
                    sp.dma_start(out[:, bass.ds(i - FFN1, 1), :, :].rearrange("b o t c -> t (o b) c"), otok[:]
                                 ).then_inc(s_out, 16)
                for done in (pe_done, act_done, dve_done, pool_done):
                    sp.wait_ge(done, i + 1)
                if FFN1 in on:
                    sp.wait_ge(s_out, loads_by(c[FFN1], 1, 1))
                sp.sem_inc(s_release, 1)

            pipeline(sp, iteration)

        @block.gpsimd
        def _(pool):
            g = nc.gpsimd
            g.memset(ident[:], 0.0).then_inc(s_setup_pool, 1)
            pool.wait_ge(s_setup_pool, 1)
            g.affine_select(out=ident[:], in_=ident[:], compare_op=ALU.not_equal, fill=1.0, base=0,
                            pattern=[[-1, P]], channel_multiplier=1).then_inc(s_setup_pool, 1)
            g.iota(iota_i[:], pattern=[[1, E]], base=0, channel_multiplier=0).then_inc(s_setup_pool, 1)
            g.memset(ones_mean[:], 1.0 / C).then_inc(s_setup_pool, 1)
            g.memset(eps[:], EPS).then_inc(s_setup_pool, 1)
            g.memset(abuf[:], 0.0).then_inc(s_setup_pool, 1)
            g.memset(hst[:], 0.0).then_inc(s_setup_pool, 1)
            pool.wait_ge(s_setup_pool, 7)

            def iteration(i, on):
                c = {s: i - s for s in on}
                def scan_operand(j):
                    q, h = divmod(j, DH)
                    if j >= DH:
                        pool.wait_ge(m_dve, at(c[MAMBA], M_DVE, f"save{j - DH}"))
                        pool.wait_ge(m_pool, at(c[MAMBA], M_POOL, f"hc{j - DH}"))
                    if h == 0:
                        pool.wait_ge(s_bcb[2 * q % 3], rows_in(c[MAMBA], 2 * q))
                    pool.wait_ge(m_dve, at(c[MAMBA], M_DVE, f"u{h}"))
                    g.tensor_tensor(bbuf[:, h, :, :, 1:], du[:, h].unsqueeze(1).to_broadcast([P, NG, B, TC]),
                                    bcb[:, 2 * q % 3].rearrange("p n (b t) -> p n b t", b=B), ALU.mult
                                    ).then_inc(m_pool, 1)
                    g.tensor_copy(bbuf[:, h, :, :, 0], hst[:, j]).then_inc(m_pool, 1)

                if MAMBA in on:
                    scan_operand(0)
                for j in range(E):
                    if MAMBA in on and j + 1 < UNITS:
                        scan_operand(j + 1)
                    if MAMBA in on:
                        q, h = divmod(j, DH)
                        if h == 0:
                            pool.wait_ge(s_bcb[(2 * q + 1) % 3], rows_in(c[MAMBA], 2 * q + 1))
                        pool.wait_ge(m_dve, at(c[MAMBA], M_DVE, f"scan{j}"))
                        g.tensor_tensor(abuf[:, h, :, :, 1:], bbuf[:, h, :, :, 1:],
                                        bcb[:, (2 * q + 1) % 3].rearrange("p n (b t) -> p n b t", b=B), ALU.mult
                                        ).then_inc(m_pool, 1)
                    for l, s in layers(on):
                        pool.wait_ge(f_dve[l], at(c[FFN[l]], F_DVE[l], f"t{j}"))
                        if j:
                            pool.wait_ge(f_pool[l], at(c[FFN[l]], F_POOL[l], f"acc{j - 1}"))
                        pool.sem_inc(s_adding[l], 1)
                        acc = X[:, bass.ds(i - s, 1), :].squeeze(1)
                        g.tensor_tensor(acc, acc, t1[l][:], ALU.add).then_inc(f_pool[l], 1)
                meet(pool, pool_done, i)

            pipeline(pool, iteration)

        @block.tensor
        def _(pe):
            mm = nc.tensor.matmul

            pe.wait_ge(s_setup_pool, 2)
            pe.wait_ge(s_wtok, n_tok)
            for k in range(4):
                last = nc.tensor.transpose(A0[:, k * P:(k + 1) * P], win_tok[:, k, :], ident[:])
            last.then_inc(s_setup_pe, 1)
            for h in range(DH):
                for o in range(DH):
                    last = nc.tensor.transpose(A1[:, h * DI + o * P:h * DI + (o + 1) * P],
                                               wdt_tok[:, o, h * P:(h + 1) * P], ident[:])
            last.then_inc(s_setup_pe, 1)
            for h in range(DH):
                last = nc.tensor.transpose(M0[:, h * 2 * NS:(h + 1) * 2 * NS],
                                           wbc_tok[:, h * P:(h + 1) * P], ident[0:2 * NS, 0:2 * NS])
            last.then_inc(s_setup_pe, 1)
            for h in range(DH):
                last = nc.tensor.transpose(M1[:, h * C:(h + 1) * C], wout_tok[:, h * P:(h + 1) * P], ident[:])
            last.then_inc(s_setup_pe, 1)
            pe.wait_ge(s_setup_act, 4)
            pe.wait_ge(s_load, n_load)
            pe.wait_ge(s_setup_pool, 4)
            pe.wait_ge(s_setup_dve, 6)

            def iteration(i, on):
                c = {s: i - s for s in on}
                R, M = RWKV in on, MAMBA in on
                chunk = {s: X[:, bass.ds(c[s], 1), :].squeeze(1) for s in on}

                def average(ps, src, s):
                    mm(ps[:], ones_mean[:], src, start=True, stop=True).then_inc(s, 1)

                if R:
                    pe.wait_ge(s_x, loads_by(c[RWKV], 1, 1))
                    for b in range(B):
                        last = nc.tensor.transpose(A0[:, b * TC:(b + 1) * TC], xtok[:, b, :], ident[:])
                    last.then_inc(r_pe, 1)
                if M:
                    average(M0, chunk[MAMBA], m_pe)
                for l, s in layers(on):
                    average(OB[l], chunk[s], f_pe[l])
                if R:
                    pe.wait_ge(r_act, at(c[RWKV], R_ACT, "xin"))
                    average(A1, xin[:], r_pe)
                if M:
                    pe.wait_ge(m_act, at(c[MAMBA], M_ACT, "sq"))
                    average(M0, sq_m, m_pe)
                for l, s in layers(on):
                    pe.wait_ge(f_act[l], at(c[FFN[l]], F_ACT[l], "sq"))
                    average(OB[l], hid[l][:, 0, :], f_pe[l])
                if R:
                    pe.wait_ge(r_act, at(c[RWKV], R_ACT, "sq0"))
                    average(A1, sq_r[:], r_pe)
                if M:
                    pe.wait_ge(m_dve, at(c[MAMBA], M_DVE, "xn"))
                    mm(M1[:], WinT[:, 0:P], rs_m[:], start=True, stop=True).then_inc(m_pe, 1)
                    mm(M0[:], WinT[:, P:2 * P], rs_m[:], start=True, stop=True).then_inc(m_pe, 1)
                if R:
                    pe.wait_ge(r_dve, at(c[RWKV], R_DVE, "x0"))
                    average(A0, x0[:], r_pe)
                if M:
                    pe.wait_ge(m_act, at(c[MAMBA], M_ACT, "xs1"))
                    for h in range(DH):
                        last = mm(M1[0:2 * NS, :], WbcT[:, h, :], xs[:, h], start=(h == 0), stop=(h == DH - 1))
                    last.then_inc(m_pe, 1)
                    for o, ps in ((0, M0), (1, M1)):
                        if o:
                            pe.wait_ge(m_act, at(c[MAMBA], M_ACT, "bc"))
                        for h in range(DH):
                            last = mm(ps[:], WdtT[:, h, o * P:(o + 1) * P], xs[:, h],
                                      start=(h == 0), stop=(h == DH - 1))
                        last.then_inc(m_pe, 1)
                if R:
                    pe.wait_ge(r_act, at(c[RWKV], R_ACT, "sq1"))
                    average(A0, sq_r[:], r_pe)

                def router(l):
                    pe.wait_ge(f_dve[l], at(c[FFN[l]], F_DVE[l], "xn"))
                    for k in range(HB):
                        if k >= 2:
                            pe.wait_ge(f_act[l], at(c[FFN[l]], F_ACT[l], f"sr{k - 2}"))
                        elif l and FFN0 in on:
                            pe.wait_ge(f_act[0], at(c[FFN0], F_ACT[0], f"sr{k + 2}"))
                        mm((H0, H1)[k % 2][:], rw1[:, k * P:(k + 1) * P], xf[l][:], start=True, stop=True
                           ).then_inc(f_pe[l], 1)

                if FFN0 in on:
                    router(0)
                if M:
                    for h, ps in ((0, M0), (1, M1)):
                        pe.wait_ge(m_act, at(c[MAMBA], M_ACT, f"ab{h}"))
                        pe.wait_ge(m_dve, at(c[MAMBA], M_DVE, f"mx{h}"))
                        mm(ps[:], WinT[:, (DH + h) * P:(DH + h + 1) * P], rs_m[:], start=True, stop=True
                           ).then_inc(m_pe, 1)
                if FFN1 in on:
                    router(1)
                for l, s in layers(on):
                    pe.wait_ge(f_act[l], at(c[FFN[l]], F_ACT[l], "sr3"))
                    for b in range(B):
                        for k in range(HB):
                            last = mm(OB[l][:, b * E:(b + 1) * E], hid[l][:, k, b * TC:(b + 1) * TC], rw2[:, k, :],
                                      start=(k == 0), stop=(k == HB - 1))
                    last.then_inc(f_pe[l], 1)
                if R:
                    pe.wait_ge(r_act, at(c[RWKV], R_ACT, "h"))
                    mm(A1[:], Wk[:], hs1[:, :, 0:TC], start=True, stop=True).then_inc(r_pe, 1)
                    mm(A0[:], Wv[:], hs1[:, :, 0:TC], start=True, stop=True).then_inc(r_pe, 1)
                    pe.wait_ge(r_act, at(c[RWKV], R_ACT, "k"))
                    mm(A1[:], Wr[:], hs1[:, :, 0:TC], start=True, stop=True).then_inc(r_pe, 1)
                for l, s in layers(on):
                    pe.wait_ge(f_dve[l], at(c[FFN[l]], F_DVE[l], "we"))
                    for b in range(B):
                        last = nc.tensor.transpose(OB[l][0:E, b * TC:(b + 1) * TC], we[l][:, b, :], ident[:])
                    last.then_inc(f_pe[l], 1)
                if M:
                    pe.wait_ge(m_act, at(c[MAMBA], M_ACT, "sz1"))
                for e in range(E):
                    for l, s in layers(on):
                        for k in range(HB):
                            if k >= 2:
                                pe.wait_ge(f_act[l], at(c[FFN[l]], F_ACT[l], f"h{e}_{k - 2}"))
                            elif e:
                                pe.wait_ge(f_act[l], at(c[FFN[l]], F_ACT[l], f"h{e - 1}_{k + 2}"))
                            mm(HR[l][k % 2][:], w1[:, e, k * P:(k + 1) * P], xf[l][:], start=True, stop=True
                               ).then_inc(f_pe[l], 1)
                    for l, s in layers(on):
                        if e:
                            pe.wait_ge(f_dve[l], at(c[FFN[l]], F_DVE[l], f"t{e - 1}"))
                        else:
                            pe.wait_ge(f_act[l], at(c[FFN[l]], F_ACT[l], "weT"))
                        for k in range(HB):
                            pe.wait_ge(f_act[l], at(c[FFN[l]], F_ACT[l], f"h{e}_{k}"))
                            last = mm(OB[l][:], w2[:, e, k, :], hid[l][:, k, :], start=(k == 0), stop=(k == HB - 1))
                        last.then_inc(f_pe[l], 1)
                if M:
                    for h in range(DH):
                        pe.wait_ge(m_dve, at(c[MAMBA], M_DVE, f"yz{h}"))
                        last = mm(M0[:], WoutT[:, h, :], ya[:, h, :], start=(h == 0), stop=(h == DH - 1))
                    last.then_inc(m_pe, 1)
                if FFN1 in on:
                    pe.wait_ge(f_act[1], at(c[FFN1], F_ACT[1], "xo"))
                    for b in range(B):
                        last = nc.tensor.transpose(H0[:, b * C:(b + 1) * C], xo[:, b * TC:(b + 1) * TC], ident[:])
                    last.then_inc(f_pe[1], 1)
                if R:
                    pe.wait_ge(r_act, at(c[RWKV], R_ACT, "tr"))
                    pe.wait_ge(r_dve, at(c[RWKV], R_DVE, "x1"))
                    average(A0, x0[:], r_pe)
                    pe.wait_ge(r_act, at(c[RWKV], R_ACT, "sq2"))
                    average(A0, sq_r[:], r_pe)
                    pe.wait_ge(r_act, at(c[RWKV], R_ACT, "h2"))
                    for k in range(HB):
                        if k >= 2:
                            pe.wait_ge(r_act, at(c[RWKV], R_ACT, f"relu{k - 2}"))
                        mm((A1, A0)[k % 2][:], Wck[:, k * P:(k + 1) * P], hs2[:, :, 0:TC], start=True, stop=True
                           ).then_inc(r_pe, 1)
                    pe.wait_ge(r_act, at(c[RWKV], R_ACT, "relu2"))
                    for k in range(HB):
                        pe.wait_ge(r_act, at(c[RWKV], R_ACT, f"kk{k}"))
                        last = mm(A1[:], Wcv[:, k, :], kk[:, k, :], start=(k == 0), stop=(k == HB - 1))
                    last.then_inc(r_pe, 1)
                    mm(A0[:], Wcr[:], hs2[:, :, 0:TC], start=True, stop=True).then_inc(r_pe, 1)
                meet(pe, pe_done, i)

            pipeline(pe, iteration)

        @block.scalar
        def _(act):
            f = nc.scalar.activation

            act.wait_ge(s_setup_pe, 4)
            nc.scalar.copy(WinT[:], A0[:]).then_inc(s_setup_act, 1)
            nc.scalar.copy(WdtT[:].rearrange("p h d -> p (h d)"), A1[:]).then_inc(s_setup_act, 1)
            nc.scalar.copy(WbcT[:].rearrange("p h n -> p (h n)"), M0[:, 0:DH * 2 * NS]).then_inc(s_setup_act, 1)
            nc.scalar.copy(WoutT[:].rearrange("p h c -> p (h c)"), M1[:, 0:DH * C]).then_inc(s_setup_act, 1)
            nc.scalar.preload_act_table_set(STATS)
            act.wait_ge(s_load, n_load)
            f(Aneg[:], Aneg[:], ACT.Exp).then_inc(s_setup_act, 1)
            f(cols[:, EU:EU + 1], cols[:, U_COL:U_COL + 1], ACT.Exp).then_inc(s_setup_act, 1)
            f(gate[:], gate[:], ACT.Exp, scale=-1.0).then_inc(s_setup_act, 1)
            act.wait_ge(s_setup_dve, 8)
            act.wait_ge(s_setup_pool, 6)

            def iteration(i, on):
                c = {s: i - s for s in on}
                R, M = RWKV in on, MAMBA in on

                def rstd(var, dst, s, done, ln, chunk):
                    f(dst, var, ACT.Ln, bias=eps[:]).then_inc(s, 1)
                    act.wait_ge(s, at(chunk, done, ln))
                    f(dst, dst, ACT.Exp, scale=-0.5).then_inc(s, 1)

                nc.scalar.preload_act_table_set(STATS)
                if R:
                    act.wait_ge(r_pe, at(c[RWKV], R_PE, "xT"))
                    nc.scalar.copy(xin[:], A0[:]).then_inc(r_act, 1)
                if M:
                    act.wait_ge(m_dve, at(c[MAMBA], M_DVE, "xc"))
                    f(sq_m, xc_m[:], ACT.Square).then_inc(m_act, 1)
                for l, s in layers(on):
                    act.wait_ge(f_dve[l], at(c[FFN[l]], F_DVE[l], "xc"))
                    f(hid[l][:, 0, :], xf[l][:], ACT.Square).then_inc(f_act[l], 1)
                if R:
                    act.wait_ge(r_dve, at(c[RWKV], R_DVE, "xc0"))
                    f(sq_r[:], xc_r[:], ACT.Square).then_inc(r_act, 1)
                if M:
                    act.wait_ge(m_pe, at(c[MAMBA], M_PE, "var"))
                    rstd(M0[:], rs_m[:], m_act, M_ACT, "ln", c[MAMBA])
                for l, s in layers(on):
                    act.wait_ge(f_pe[l], at(c[FFN[l]], F_PE[l], "var"))
                    rstd(OB[l][:], t1[l][:], f_act[l], F_ACT[l], "ln", c[s])
                if R:
                    act.wait_ge(r_pe, at(c[RWKV], R_PE, "var0"))
                    rstd(A1[:], rs_r[:], r_act, R_ACT, "ln0", c[RWKV])
                if M:
                    for h, ps in ((0, M1), (1, M0)):
                        act.wait_ge(m_pe, at(c[MAMBA], M_PE, f"xs{h}"))
                        nc.scalar.copy(xs[:, h].rearrange("p b t -> p (b t)"), ps[:]).then_inc(m_act, 1)
                if R:
                    act.wait_ge(r_dve, at(c[RWKV], R_DVE, "xc1"))
                    f(sq_r[:], xc_r[:], ACT.Square).then_inc(r_act, 1)
                if M:
                    act.wait_ge(m_pe, at(c[MAMBA], M_PE, "bc"))
                    nc.scalar.copy(bcs, M1[0:2 * NS, :]).then_inc(m_act, 1)
                if R:
                    act.wait_ge(r_pe, at(c[RWKV], R_PE, "var1"))
                    rstd(A0[:], rs_r[:], r_act, R_ACT, "ln1", c[RWKV])
                if M:
                    for h, ps in ((0, M0), (1, M1)):
                        act.wait_ge(m_pe, at(c[MAMBA], M_PE, f"dt{h}"))
                        f(dt[:, h, :], ps[:], ACT.Abs, bias=bdt[:, h:h + 1]).then_inc(m_act, 1)
                    for h in range(DH):
                        act.wait_ge(m_act, at(c[MAMBA], M_ACT, f"ab{h}"))
                        f(dt[:, h, :], dt[:, h, :], ACT.Exp, scale=-1.0).then_inc(m_act, 1)
                    for h in range(DH):
                        act.wait_ge(m_act, at(c[MAMBA], M_ACT, f"ex{h}"))
                        f(ya[:, h, :], dt[:, h, :], ACT.Ln, bias=1.0).then_inc(m_act, 1)
                if R:
                    act.wait_ge(r_dve, at(c[RWKV], R_DVE, "xn1"))
                    f(hs1[:, :, 1:], xc_r[:].rearrange("p (b t) -> p b t", b=B), ACT.Identity,
                      bias=cols[:, B1:B1 + 1], scale=cols[:, G1:G1 + 1]).then_inc(r_act, 1)
                if M or layers(on):
                    nc.scalar.preload_act_table_set(SILU)

                def router(l):
                    for k in range(HB):
                        act.wait_ge(f_pe[l], at(c[FFN[l]], F_PE[l], f"r{k}"))
                        f(hid[l][:, k, :], (H0, H1)[k % 2][:], ACT.Silu, bias=rb1[:, k:k + 1]).then_inc(f_act[l], 1)

                if FFN0 in on:
                    router(0)
                if M:
                    for h, ps in ((0, M0), (1, M1)):
                        act.wait_ge(m_dve, at(c[MAMBA], M_DVE, f"dt{h}"))
                        act.wait_ge(m_pe, at(c[MAMBA], M_PE, f"z{h}"))
                        f(sz[:, h, :], ps[:], ACT.Silu).then_inc(m_act, 1)
                if FFN1 in on:
                    router(1)
                nc.scalar.preload_act_table_set(STATS)
                for l, s in layers(on):
                    act.wait_ge(f_dve[l], at(c[FFN[l]], F_DVE[l], "d"))
                    f(gp[l][:, 1, :], gp[l][:, 0, :], ACT.Exp).then_inc(f_act[l], 1)
                if R:
                    act.wait_ge(r_pe, at(c[RWKV], R_PE, "k"))
                    nc.scalar.copy(kb[:, :, 1:], A1[:].rearrange("p (b t) -> p b t", b=B)).then_inc(r_act, 1)
                    act.wait_ge(r_pe, at(c[RWKV], R_PE, "v"))
                    nc.scalar.copy(vb[:].rearrange("p b t -> p (b t)"), A0[:]).then_inc(r_act, 1)
                    act.wait_ge(r_dve, at(c[RWKV], R_DVE, "dkc"))
                    f(gam[:], gam[:], ACT.Exp).then_inc(r_act, 1)
                for l, s in layers(on):
                    act.wait_ge(f_pe[l], at(c[FFN[l]], F_PE[l], "weT"))
                    nc.scalar.copy(weT[l], OB[l][0:E, :]).then_inc(f_act[l], 1)

                def decays(j):
                    q, h = divmod(j, DH)
                    nc.scalar.preload_act_table_set(STATS)
                    act.wait_ge(m_dve, at(c[MAMBA], M_DVE, f"dt{h}" if j < DH else f"red{j - DH}"))
                    for n in range(NG):
                        f(abuf[:, h, n, :, 1:], dt[:, h, :].rearrange("p (b t) -> p b t", b=B), ACT.Exp,
                          scale=Aneg[:, h, q * NG + n:q * NG + n + 1]).then_inc(m_act, 1)

                if M:
                    decays(0)
                if R:
                    nc.scalar.preload_act_table_set(SILU)
                    act.wait_ge(r_pe, at(c[RWKV], R_PE, "r"))
                    f(tr[:], A1[:], ACT.Tanh, scale=0.5).then_inc(r_act, 1)
                for e in range(E):
                    if layers(on):
                        nc.scalar.preload_act_table_set(SILU)
                    for l, s in layers(on):
                        if e == 0:
                            act.wait_ge(f_pe[l], at(c[FFN[l]], F_PE[l], "logits"))
                        for k in range(HB):
                            act.wait_ge(f_pe[l], at(c[FFN[l]], F_PE[l], f"h{e}_{k}"))
                            f(hid[l][:, k, :], HR[l][k % 2][:], ACT.Silu, bias=b1[:, e, k:k + 1]).then_inc(f_act[l], 1)
                    if M and e + 1 < UNITS:
                        decays(e + 1)
                if FFN1 in on:
                    act.wait_ge(f_pool[1], at(c[FFN1], F_POOL[1], f"acc{E - 1}"))
                    nc.scalar.copy(xo[:], X[:, bass.ds(i - FFN1, 1), :].squeeze(1)).then_inc(f_act[1], 1)
                    act.wait_ge(f_pe[1], at(c[FFN1], F_PE[1], "oT"))
                    nc.scalar.copy(otok[:].rearrange("p b c -> p (b c)"), H0[:]).then_inc(f_act[1], 1)
                if R:
                    act.wait_ge(r_dve, at(c[RWKV], R_DVE, "xc2"))
                    f(sq_r[:], xc_r[:], ACT.Square).then_inc(r_act, 1)
                    nc.scalar.preload_act_table_set(STATS)
                    act.wait_ge(r_pe, at(c[RWKV], R_PE, "var2"))
                    rstd(A0[:], rs_r[:], r_act, R_ACT, "ln2", c[RWKV])
                    act.wait_ge(r_dve, at(c[RWKV], R_DVE, "xn2"))
                    f(hs2[:, :, 1:], xc_r[:].rearrange("p (b t) -> p b t", b=B), ACT.Identity,
                      bias=cols[:, B2:B2 + 1], scale=cols[:, G2:G2 + 1]).then_inc(r_act, 1)
                    if FFN0 in on:
                        act.wait_ge(f_pe[0], at(c[FFN0], F_PE[0], f"out{E - 1}"))
                    for k in range(HB):
                        act.wait_ge(r_pe, at(c[RWKV], R_PE, f"ck{k}"))
                        f(kk[:, k, :], (A1, A0)[k % 2][:], ACT.Relu).then_inc(r_act, 1)
                        act.wait_ge(r_act, at(c[RWKV], R_ACT, f"relu{k}"))
                        f(kk[:, k, :], kk[:, k, :], ACT.Square).then_inc(r_act, 1)
                    nc.scalar.preload_act_table_set(SILU)
                    act.wait_ge(r_pe, at(c[RWKV], R_PE, "cr"))
                    f(tr[:], A0[:], ACT.Tanh, scale=0.5).then_inc(r_act, 1)
                meet(act, act_done, i)

            pipeline(act, iteration)

        @block.vector
        def _(dve):
            v = nc.vector
            tt, stt, ts = v.tensor_tensor, v.scalar_tensor_tensor, v.tensor_scalar

            dve.wait_ge(s_load, n_load)
            ts_col = cols[:, TS_COL:TS_COL + 1].unsqueeze(1).to_broadcast([P, B, 1])
            v.tensor_copy(hs1[:, :, TC:], ts_col).then_inc(s_setup_dve, 1)
            v.tensor_copy(hs2[:, :, TC:], ts_col).then_inc(s_setup_dve, 1)
            v.memset(kb[:, :, TC:], -1e4).then_inc(s_setup_dve, 1)
            v.memset(aab[:, :, TC:], 0.0).then_inc(s_setup_dve, 1)
            v.memset(pb[:, :, TC:], 0.0).then_inc(s_setup_dve, 1)
            v.memset(cb[:, :, TC:], 1.0).then_inc(s_setup_dve, 1)
            dve.wait_ge(s_setup_act, 7)
            ts(gate[:], gate[:], 1.0, None, ALU.add).then_inc(s_setup_dve, 1)
            ts(Aneg[:], Aneg[:], -1.0, None, ALU.mult).then_inc(s_setup_dve, 1)
            dve.wait_ge(s_setup_dve, 7)
            v.reciprocal(gate[:], gate[:]).then_inc(s_setup_dve, 1)
            dve.wait_ge(s_setup_pool, 7)
            v.tensor_copy(iota_f[:], iota_i[:]).then_inc(s_setup_dve, 1)
            dve.wait_ge(s_setup_dve, 10)

            def iteration(i, on):
                c = {s: i - s for s in on}
                R, M = RWKV in on, MAMBA in on
                chunk = {s: X[:, bass.ds(c[s], 1), :].squeeze(1) for s in on}

                def gates_1(l):
                    dve.wait_ge(f_pe[l], at(c[FFN[l]], F_PE[l], "logits"))
                    tt(lg[l][:], OB[l][:, 0:B * E].rearrange("p (b e) -> p b e", b=B),
                       rb2[:].unsqueeze(1).to_broadcast([P, B, E]), ALU.add).then_inc(s_top[l], 1)
                    dve.wait_ge(s_top[l], 1)
                    for b in range(B):
                        v.max(top[l][:, b, :], lg[l][:, b, :]).then_inc(s_top[l], 1)
                    for b in range(B):
                        dve.wait_ge(s_top[l], 2 + b)
                        v.max_index(idx[l][:, b, :], top[l][:, b, :], lg[l][:, b, :]).then_inc(s_top[l], 1)
                    dve.wait_ge(s_top[l], 1 + 2 * B)
                    v.tensor_copy(idf[l][:], idx[l][:]).then_inc(f_dve[l], 1)
                    tt(gp[l][:, 0, :], top[l][:, :, 1], top[l][:, :, 0], ALU.subtract).then_inc(f_dve[l], 1)

                def gates_2(l):
                    g = gp[l]
                    dve.wait_ge(f_act[l], at(c[FFN[l]], F_ACT[l], "gex"))
                    ts(g[:, 2, :], g[:, 1, :], 1.0, None, ALU.add).then_inc(f_dve[l], 1)
                    dve.wait_ge(f_dve[l], at(c[FFN[l]], F_DVE[l], "den"))
                    v.reciprocal(g[:, 3, :], g[:, 2, :]).then_inc(f_dve[l], 1)
                    dve.wait_ge(f_dve[l], at(c[FFN[l]], F_DVE[l], "p0"))
                    tt(g[:, 4, :], g[:, 1, :], g[:, 3, :], ALU.mult).then_inc(f_dve[l], 1)
                    for k in range(TOPK):
                        m = mk[l][:, k]
                        tt(m, iota_f[:].unsqueeze(1).to_broadcast([P, B, E]),
                           idf[l][:, :, k:k + 1].to_broadcast([P, B, E]), ALU.is_equal).then_inc(f_dve[l], 1)
                        dve.wait_ge(f_dve[l], at(c[FFN[l]], F_DVE[l], f"m{k}"))
                        tt(m, m, g[:, 3 + k, :].unsqueeze(2).to_broadcast([P, B, E]), ALU.mult).then_inc(f_dve[l], 1)
                    dve.wait_ge(f_dve[l], at(c[FFN[l]], F_DVE[l], "w1"))
                    tt(we[l], mk[l][:, 0], mk[l][:, 1], ALU.add).then_inc(f_dve[l], 1)

                def wkv_step(t):
                    r, p, c = rb[:, :, t], pb[:, :, t], cb[:, :, t]
                    bb = bbs[:, t % 2]
                    if t:
                        dve.wait_ge(s_wkv, 5 * t - 1)
                    stt(out=r, in0=p, scalar=1.0, in1=gam[:, :, t], op0=ALU.add, op1=ALU.mult).then_inc(s_wkv, 1)
                    if t:
                        dve.wait_ge(s_wkv, 5 * t)
                    stt(out=bb, in0=p, scalar=1.0, in1=c, op0=ALU.add, op1=ALU.mult).then_inc(s_wkv, 1)
                    dve.wait_ge(s_wkv, 5 * t + 1)
                    v.reciprocal(rcp[:], r).then_inc(s_wkv, 1)
                    dve.wait_ge(s_wkv, 5 * t + 2)
                    stt(out=pb[:, :, t + 1], in0=r, scalar=R_MAX, in1=bb, op0=ALU.min, op1=ALU.mult).then_inc(s_wkv, 1)
                    dve.wait_ge(s_wkv, 5 * t + 3)
                    ts(cb[:, :, t + 1], rcp[:], 1.0, 1.0 / R_MAX, ALU.min, ALU.max).then_inc(s_wkv, 1)

                if R:
                    for buf in (hs1, hs2, kb, aab, pb, cb):
                        v.tensor_copy(buf[:, :, 0:1], buf[:, :, TC:]).then_inc(r_dve, 1)
                if M:
                    dve.wait_ge(m_pe, at(c[MAMBA], M_PE, "mean"))
                    tt(xc_m[:], chunk[MAMBA], M0[:], ALU.subtract).then_inc(m_dve, 1)
                for l, s in layers(on):
                    dve.wait_ge(f_pe[l], at(c[FFN[l]], F_PE[l], "mean"))
                    tt(xf[l][:], chunk[s], OB[l][:], ALU.subtract).then_inc(f_dve[l], 1)
                if R:
                    dve.wait_ge(r_act, at(c[RWKV], R_ACT, "xin"))
                    dve.wait_ge(r_pe, at(c[RWKV], R_PE, "mean0"))
                    tt(xc_r[:], xin[:], A1[:], ALU.subtract).then_inc(r_dve, 1)
                if M:
                    dve.wait_ge(m_act, at(c[MAMBA], M_ACT, "rstd"))
                    tt(rs_m[:], xc_m[:], rs_m[:], ALU.mult).then_inc(m_dve, 1)
                for l, s in layers(on):
                    dve.wait_ge(f_act[l], at(c[FFN[l]], F_ACT[l], "rstd"))
                    tt(xf[l][:], xf[l][:], t1[l][:], ALU.mult).then_inc(f_dve[l], 1)
                if R:
                    dve.wait_ge(r_act, at(c[RWKV], R_ACT, "rstd0"))
                    tt(x0[:], xc_r[:], rs_r[:], ALU.mult).then_inc(r_dve, 1)
                    dve.wait_ge(r_pe, at(c[RWKV], R_PE, "mean1"))
                    tt(xc_r[:], x0[:], A0[:], ALU.subtract).then_inc(r_dve, 1)
                    dve.wait_ge(r_act, at(c[RWKV], R_ACT, "rstd1"))
                    tt(xc_r[:], xc_r[:], rs_r[:], ALU.mult).then_inc(r_dve, 1)
                if M:
                    for h, ps in ((0, M0), (1, M1)):
                        dve.wait_ge(m_act, at(c[MAMBA], M_ACT, f"ab{h}"))
                        ts(mx[:, h, :], ps[:], bdt[:, h:h + 1], 0.0, ALU.add, ALU.max).then_inc(m_dve, 1)
                    dus = [du[:, h].rearrange("p b t -> p (b t)") for h in range(DH)]
                    for k, coef in enumerate((-4.0 / 3.0, 2.0, -4.0)):
                        for h in range(DH):
                            if k == 0:
                                dve.wait_ge(m_act, at(c[MAMBA], M_ACT, f"ex{h}"))
                            else:
                                dve.wait_ge(m_dve, at(c[MAMBA], M_DVE, f"p{k - 1}{h}"))
                            stt(out=dus[h], in0=dus[h] if k else dt[:, h, :], scalar=coef, in1=dt[:, h, :],
                                op0=ALU.add, op1=ALU.mult).then_inc(m_dve, 1)
                    for h in range(DH):
                        dve.wait_ge(m_act, at(c[MAMBA], M_ACT, f"lp{h}"))
                        stt(out=ya[:, h, :], in0=dt[:, h, :], scalar=LN_FROM, in1=ya[:, h, :],
                            op0=ALU.is_ge, op1=ALU.mult).then_inc(m_dve, 1)
                    for h in range(DH):
                        dve.wait_ge(m_dve, at(c[MAMBA], M_DVE, f"g{h}"))
                        stt(out=dus[h], in0=dus[h], scalar=-0.25, in1=ya[:, h, :],
                            op0=ALU.mult, op1=ALU.max).then_inc(m_dve, 1)
                    for h in range(DH):
                        dve.wait_ge(m_dve, at(c[MAMBA], M_DVE, f"lc{h}"))
                        tt(dt[:, h, :], dus[h], mx[:, h, :], ALU.add).then_inc(m_dve, 1)
                    for h in range(DH):
                        dve.wait_ge(m_dve, at(c[MAMBA], M_DVE, f"dt{h}"))
                        tt(dus[h], dt[:, h, :],
                           xs[:, h].rearrange("p b t -> p (b t)"), ALU.mult).then_inc(m_dve, 1)
                for l, s in layers(on):
                    gates_1(l)
                if R:
                    dve.wait_ge(r_act, at(c[RWKV], R_ACT, "k"))
                    stt(out=gam[:], in0=kb[:, :, 0:TC], scalar=cols[:, W_COL:W_COL + 1], in1=kb[:, :, 1:],
                        op0=ALU.add, op1=ALU.subtract).then_inc(r_dve, 1)
                    dve.wait_ge(r_dve, at(c[RWKV], R_DVE, "dk"))
                    ts(gam[:], gam[:], G_MAX, G_MIN, ALU.min, ALU.max).then_inc(r_dve, 1)
                for l, s in layers(on):
                    gates_2(l)
                if R:
                    dve.wait_ge(r_act, at(c[RWKV], R_ACT, "gamma"))

                for j in range(E):
                    q, h = divmod(j, DH)
                    if M:
                        dve.wait_ge(m_act, at(c[MAMBA], M_ACT, f"exp{j}_{NG - 1}"))
                        dve.wait_ge(m_pool, at(c[MAMBA], M_POOL, f"edge{j}"))
                        flat = [x[:, h].rearrange("p n b t -> p (n b t)") for x in (abuf, bbuf)]
                        v.tensor_tensor_scan(flat[1], flat[0], flat[1], 0.0, ALU.mult, ALU.add).then_inc(m_dve, 1)
                        dve.wait_ge(m_dve, at(c[MAMBA], M_DVE, f"scan{j}"))
                        v.tensor_copy(hst[:, j], bbuf[:, h, :, :, TC]).then_inc(m_dve, 1)
                    if R:
                        for t in range(j * STEPS, (j + 1) * STEPS):
                            wkv_step(t)
                    if M:
                        dve.wait_ge(m_pool, at(c[MAMBA], M_POOL, f"hc{j}"))
                        dst = ya[:, h, :] if q == 0 else yr[:]
                        v.tensor_reduce(dst.rearrange("p (b t) -> p b t", b=B),
                                        abuf[:, h, :, :, 1:].rearrange("p n b t -> p b t n"), AX.X, ALU.add
                                        ).then_inc(m_dve, 1)
                        dve.wait_ge(m_dve, at(c[MAMBA], M_DVE, f"red{j}"))
                        if q:
                            tt(ya[:, h, :], ya[:, h, :], yr[:], ALU.add).then_inc(m_dve, 1)
                    for l, s in layers(on):
                        dve.wait_ge(f_pe[l], at(c[FFN[l]], F_PE[l], f"out{j}"))
                        dve.wait_ge(s_wb[l][j % 2], loads_by(c[s], E // 2, j // 2 + 1))
                        if j:
                            dve.wait_ge(f_pool[l], at(c[FFN[l]], F_POOL[l], f"acc{j - 1}"))
                        stt(out=t1[l][:], in0=OB[l][:], scalar=b2[:, j:j + 1], in1=wb[l][:, j % 2, :],
                            op0=ALU.add, op1=ALU.mult).then_inc(f_dve[l], 1)
                if M:
                    dve.wait_ge(m_dve, at(c[MAMBA], M_DVE, f"acc{UNITS - 1}"))
                    for h in range(DH):
                        stt(out=ya[:, h, :], in0=xs[:, h].rearrange("p b t -> p (b t)"), scalar=Dp[:, h:h + 1],
                            in1=ya[:, h, :], op0=ALU.mult, op1=ALU.add).then_inc(m_dve, 1)
                    for h in range(DH):
                        dve.wait_ge(m_dve, at(c[MAMBA], M_DVE, f"y{h}"))
                        dve.wait_ge(m_act, at(c[MAMBA], M_ACT, f"sz{h}"))
                        tt(ya[:, h, :], ya[:, h, :], sz[:, h, :], ALU.mult).then_inc(m_dve, 1)
                if R:
                    num, den = sq_r[:].rearrange("p (b t) -> p b t", b=B), rs_r[:].rearrange("p (b t) -> p b t", b=B)
                    rm = kb[:, :, 0:TC]
                    eu = cols[:, EU:EU + 1]
                    dve.wait_ge(s_wkv, 5 * TC)
                    ts(rm, rb[:], 1.0, None, ALU.min).then_inc(r_dve, 1)
                    tt(gam[:], vb[:], cb[:, :, 1:], ALU.mult).then_inc(r_dve, 1)
                    dve.wait_ge(r_dve, at(c[RWKV], R_DVE, "vc"))
                    for b in range(B):
                        v.tensor_tensor_scan(aab[:, b, 1:], rm[:, b, :], gam[:, b, :], aab[:, b, 0:1],
                                             ALU.mult, ALU.add).then_inc(r_dve, 1)
                    dve.wait_ge(r_dve, at(c[RWKV], R_DVE, "aa3"))
                    stt(out=num, in0=rb[:], scalar=R_MAX, in1=aab[:, :, 0:TC], op0=ALU.min, op1=ALU.mult
                        ).then_inc(r_dve, 1)
                    ts(den, pb[:, :, 1:], eu, None, ALU.add).then_inc(r_dve, 1)
                    dve.wait_ge(r_dve, at(c[RWKV], R_DVE, "den"))
                    v.reciprocal(den, den).then_inc(r_dve, 1)
                    stt(out=num, in0=vb[:], scalar=eu, in1=num, op0=ALU.mult, op1=ALU.add).then_inc(r_dve, 1)
                    dve.wait_ge(r_dve, at(c[RWKV], R_DVE, "num"))
                    tt(num, num, den, ALU.mult).then_inc(r_dve, 1)
                    dve.wait_ge(r_dve, at(c[RWKV], R_DVE, "y"))
                    dve.wait_ge(r_act, at(c[RWKV], R_ACT, "tr"))
                    stt(out=sq_r[:], in0=tr[:], scalar=1.0, in1=sq_r[:], op0=ALU.add, op1=ALU.mult).then_inc(r_dve, 1)
                    dve.wait_ge(r_dve, at(c[RWKV], R_DVE, "ys"))
                    stt(out=x0[:], in0=sq_r[:], scalar=0.5, in1=x0[:], op0=ALU.mult, op1=ALU.add).then_inc(r_dve, 1)
                    dve.wait_ge(r_pe, at(c[RWKV], R_PE, "mean2"))
                    tt(xc_r[:], x0[:], A0[:], ALU.subtract).then_inc(r_dve, 1)
                if M:
                    dve.wait_ge(m_pe, at(c[MAMBA], M_PE, "out"))
                    stt(out=chunk[MAMBA], in0=M0[:], scalar=gate[:], in1=chunk[MAMBA], op0=ALU.mult, op1=ALU.add
                        ).then_inc(m_dve, 1)
                if R:
                    dve.wait_ge(r_act, at(c[RWKV], R_ACT, "rstd2"))
                    tt(xc_r[:], xc_r[:], rs_r[:], ALU.mult).then_inc(r_dve, 1)
                    dve.wait_ge(r_act, at(c[RWKV], R_ACT, "trc"))
                    stt(out=tr[:], in0=tr[:], scalar=1.0, in1=A1[:], op0=ALU.add, op1=ALU.mult).then_inc(r_dve, 1)
                    dve.wait_ge(r_dve, at(c[RWKV], R_DVE, "s"))
                    stt(out=x0[:], in0=tr[:], scalar=0.5, in1=x0[:], op0=ALU.mult, op1=ALU.add).then_inc(r_dve, 1)
                    dve.wait_ge(r_dve, at(c[RWKV], R_DVE, "x2"))
                    tt(chunk[RWKV], x0[:], xin[:], ALU.add).then_inc(r_dve, 1)
                if R:
                    dve.sem_clear(s_wkv)
                for l, s in layers(on):
                    dve.sem_clear(s_top[l])
                meet(dve, dve_done, i)

            pipeline(dve, iteration)


_INS = ["L0_attn_a_x", "L0_attn_a_time_decay", "L0_attn_a_time_first", "L0_attn_a_time_shift", "L0_attn_a_Wk",
        "L0_attn_a_Wv", "L0_attn_a_Wr", "L0_attn_a_Wck", "L0_attn_a_Wcv", "L0_attn_a_Wcr", "L0_attn_a_ln1_g",
        "L0_attn_a_ln1_b", "L0_attn_a_ln2_g", "L0_attn_a_ln2_b", "L0_attn_b_W_in", "L0_attn_b_A_log",
        "L0_attn_b_W_B", "L0_attn_b_W_C", "L0_attn_b_W_dt", "L0_attn_b_b_dt", "L0_attn_b_D",
        "L0_attn_b_output_gate", "L0_attn_b_W_out", "L0_ffn_rw1", "L0_ffn_rb1", "L0_ffn_rw2", "L0_ffn_rb2",
        "L0_ffn_w1", "L0_ffn_b1", "L0_ffn_w2", "L0_ffn_b2"]
_COLUMNS = ("time_decay", "time_first", "ln1_g", "ln1_b", "ln2_g", "ln2_b")


def kernel(**inputs):
    import numpy as _np
    import concourse.bacc as _bacc
    from concourse import mybir as _mybir
    from concourse.bass_utils import run_bass_kernel_spmd as _run

    nc = _bacc.Bacc("TRN2", target_bir_lowering=False, num_devices=1)
    arrays, aps = {}, {}
    for name in _INS:
        x = _np.ascontiguousarray(inputs[name])
        arrays[f"in_{name}_dram"] = x
        ap = nc.dram_tensor(f"in_{name}_dram", x.shape, _mybir.dt.from_np(x.dtype), kind="ExternalInput").ap()
        short = name.removeprefix("L0_attn_a_").removeprefix("L0_attn_b_").removeprefix("L0_ffn_")
        if short in _COLUMNS:
            ap = ap.unsqueeze(1)
        if short == "time_shift":
            short, ap = "ts", ap.rearrange("a b c -> c (a b)")
        if short == "x":
            ap = ap.rearrange("b (n t) c -> b n t c", t=TC)
        aps[short] = ap
    out = nc.dram_tensor("out_0_dram", (B, T, C), F32, kind="ExternalOutput").ap()
    build(nc, aps, out.rearrange("b (n t) c -> b n t c", t=TC))
    r = _run(nc, [arrays], core_ids=[0])
    return _np.asarray(r.results[0]["out_0_dram"])
```

```python
from contextlib import ExitStack

import concourse.bass as bass
from concourse import mybir

F32 = mybir.dt.float32
U32 = mybir.dt.uint32
I32 = mybir.dt.int32
ALU = mybir.AluOpType
ACT = mybir.ActivationFunctionType
AX = mybir.AxisListType

P = 128
B, T, C = 4, 1024, 128
TC = 128
NCH = T // TC
N = B * TC
E, HID, TOPK = 8, 512, 2
HB = HID // P
DI, NS = 256, 16
DH = DI // P
NG = 4
Q = NS // NG
UNITS = Q * DH
R_MAX = 2.0 ** 80
G_MIN, G_MAX = -80.0, 25.0
LN_FROM = 1.0 / 32
EPS = 1e-5
STAGES = 4
RWKV, FFN0, MAMBA, FFN1 = range(STAGES)
FFN = (FFN0, FFN1)
FIRST = [RWKV]
STATS = "natural_log_exp_and_others"
SILU = "silu_and_others"


def order(*names):
    return {name: k + 1 for k, name in enumerate(names)}


def at(chunk, steps, name):
    return chunk * len(steps) + steps[name]


def loads_by(chunk, per_chunk, k):
    return 16 * (chunk * per_chunk + k)


def rows_in(chunk, k):
    return loads_by(chunk, len(range(k % 3, 2 * Q, 3)), k // 3 + 1)


def build(nc, a, out):
    assert E == UNITS and NG == 4
    STEPS = (22, 8, 8)
    STEPS += tuple((TC - sum(STEPS) + k) // (E - 2) for k in range(E - 2))
    assert sum(STEPS) == TC
    PAIRED = (0, 2, 4, 6)

    R_PE = order("xT", "cen0", "var0", "k", "v", "r", "cen2", "var2",
                 "ck0", "ck1", "ck2", "ck3", "cr", "kv")
    R_ACT = order("xin", "sq0", "ln0", "rstd0", "ln1", "rstd1", "h", "k", "v", "gamma", "tr",
                  "sq2", "ln2", "rstd2", "h2", "relu0", "kk0", "relu1", "kk1", "relu2", "kk2",
                  "relu3", "kk3", "trc")
    R_DVE = order("h", "h2", "k", "aa", "p", "c", "vr", "x0", "var1", "xn1", "dk", "dkc",
                  "rmin", "vc", "aa0", "aa1", "aa2", "aa3", "ra", "den", "rden", "num", "y", "ys",
                  "x1", "xn2", "s", "x2", "X")
    M_PE = order("cen", "var", "xs0", "xs1", "bc", "dt0", "dt1", "z0", "z1", "out")
    M_ACT = order("sq", "ln", "rstd", "xs0", "xs1", "bc", "ab0", "mx0", "ab1", "mx1", "ex0", "ex1",
                  "lp0", "lp1", "sz0", "sz1",
                  *[f"exp{j}_{n}" for j in range(UNITS) for n in range(NG)])
    M_DVE = order("xn", "p00", "p01", "p10", "p11", "p20", "p21", "g0", "g1",
                  "lc0", "lc1", "dt0", "dt1", "u0", "u1",
                  "scan0", "save0", *[s for j in range(UNITS) for s in
                    ([f"scan{j + 1}", f"save{j + 1}"] if j + 1 < UNITS else []) + [f"red{j}"]
                    + ([f"acc{j}"] if j >= DH else [])],
                  "y0", "y1", "yz0", "yz1", "X")
    M_POOL = order("bu0", "edge0", *[s for j in range(UNITS) for s in
                   ([f"bu{j + 1}", f"edge{j + 1}"] if j + 1 < UNITS else []) + [f"hc{j}"]
                   + ([f"pairs{j}"] if j in PAIRED else [])])
    F_PE = order("cen", "var", "r0", "r1", "r2", "r3", "logits",
                 *[s for e in range(E) for s in
                   [f"h{e}_{k}" for k in range(HB)] + (["weT"] if e == 0 else []) + [f"out{e}"]])
    F_PE = (F_PE, order(*F_PE, "oT"))
    F_ACT = order("sq", "ln", "rstd", "sr0", "sr1", "sr2", "sr3", "gex", *[f"h0_{k}" for k in range(HB)], "weT",
                  *[f"h{e}_{k}" for e in range(1, E) for k in range(HB)])
    F_ACT = (F_ACT, order(*F_ACT, "xo", "o"))
    F_DVE = order("xn", "idxf",
                  "d", "den", "p0", "p1", "m0", "w0", "m1", "w1", "we", *[f"t{e}" for e in range(E)])
    F_DVE = (F_DVE, F_DVE)
    F_POOL = order(*[f"acc{e}" for e in range(E)])
    F_POOL = (F_POOL, F_POOL)

    with ExitStack() as ctx:
        def sb(name, shape, dt=F32):
            return ctx.enter_context(nc.sbuf_tensor(name, shape, dt))

        def bank(name):
            return ctx.enter_context(nc.psum_tensor(name, [P, N], F32))

        def sem(name):
            return ctx.enter_context(nc.semaphore(name))

        ident = sb("ident", [P, P])
        ones_mean = sb("ones_mean", [P, P])
        centre = sb("centre", [P, P])
        eps = sb("eps", [P, 1])
        iota_i = sb("iota_i", [P, E], I32)
        iota_f = sb("iota_f", [P, E])
        Wk, Wv, Wr, Wcr = (sb(n, [P, C]) for n in ("Wk", "Wv", "Wr", "Wcr"))
        Wck = sb("Wck", [P, HID])
        Wcv = sb("Wcv", [P, HB, C])
        cols = sb("cols", [P, 8])
        W_COL, U_COL, TS_COL, G1, B1, G2, B2, EU = range(8)
        WinT = sb("WinT", [P, 2 * DI])
        WbcT = sb("WbcT", [P, DH, 2 * NS])
        WdtT = sb("WdtT", [P, DH, DI])
        WoutT = sb("WoutT", [P, DH, C])
        Aneg = sb("Aneg", [P, DH, NS])
        bdt = sb("bdt", [P, DH])
        Dp = sb("Dp", [P, DH])
        gate = sb("gate", [P, 1])
        rw1 = sb("rw1", [P, HID])
        rb1 = sb("rb1", [P, HB])
        rw2 = sb("rw2", [P, HB, E])
        rb2 = sb("rb2", [P, E])
        w1 = sb("w1", [P, E, HID])
        b1 = sb("b1", [P, E, HB])
        w2 = sb("w2", [P, E, HB, C])
        b2 = sb("b2", [P, E])

        X = sb("X", [P, NCH, N])

        xtok = sb("xtok", [P, B, C])
        xin = sb("xin", [P, N])
        x0 = sb("x0", [P, N])
        xc_r = sb("xc_r", [P, N])
        sq_r = sb("sq_r", [P, N])
        rs_r = sb("rs_r", [P, N])
        hs1 = sb("hs1", [P, B, TC + 1])
        hs2 = sb("hs2", [P, B, TC + 1])
        kb = sb("kb", [P, B, TC + 1])
        aab = sb("aab", [P, B, TC + 1])
        pb = sb("pb", [P, B, TC + 1])
        cb = sb("cb", [P, B, TC + 1])
        vb = sb("vb", [P, B, TC])
        gam = sb("gam", [P, B, TC])
        rb = sb("rb", [P, B, TC])
        bbs = sb("bbs", [P, 2, B])
        rcp = sb("rcp", [P, B])
        tr = xc_r

        rs_m = sb("rs_m", [P, N])
        xs = sb("xs", [P, DH, B, TC])
        sz = sb("sz", [P, DH, N])
        dt = sb("dt", [P, DH, N])
        du = sb("du", [P, DH, B, TC])
        ya = sb("ya", [P, DH, N])
        yr = sb("yr", [P, N])
        sq_m = ya[:, 0, :]
        bcs = yr[0:2 * NS, :]
        bcb = sb("bcb", [P, 3, NG, N])
        abuf = sb("abuf", [P, DH, NG, B, TC + 1])
        bbuf = sb("bbuf", [P, DH, NG, B, TC + 1])
        hst = sb("hst", [P, UNITS, NG, B])
        mx = [abuf[:, 1, h, :, 1:] for h in range(DH)]

        xf = [sb(f"xf{l}", [P, N]) for l in range(2)]
        t1 = [sb(f"t1_{l}", [P, N]) for l in range(2)]
        hid = [sb(f"hid{l}", [P, HB, N]) for l in range(2)]
        wb = [sb(f"wb{l}", [P, 2, N]) for l in range(2)]
        lg = [sb(f"lg{l}", [P, B, E]) for l in range(2)]
        idx = [sb(f"idx{l}", [P, B, E], U32) for l in range(2)]
        idf = lg
        gp = [sb(f"gp{l}", [P, 5, B]) for l in range(2)]
        mk = [sb(f"mk{l}", [P, 2, B, E]) for l in range(2)]
        top = [mk[l][:, 1] for l in range(2)]
        we = [mk[l][:, 0] for l in range(2)]
        weT = [t1[l][0:E, :] for l in range(2)]
        xo = xf[1]
        otok = xtok
        kk = bbuf[:, 0].rearrange("p n b t -> p (n b t)")[:, 0:HB * N].rearrange("p (k t) -> p k t", k=HB)

        we_dram = [nc.dram_tensor(f"we_scratch{l}", [E, N], F32, kind="Internal").ap() for l in range(2)]
        bc_dram = nc.dram_tensor("bc_scratch", [2, NS, N], F32, kind="Internal").ap()

        A0, A1, M0, M1, H0, H1, O0, O1 = (bank(n) for n in ("A0", "A1", "M0", "M1", "H0", "H1", "O0", "O1"))
        OB = (O0, O1)
        HV = (H0, H1)
        CK = (A1, A0, M1, H0)
        HR = ((H0, H1), (M0, M1))

        s_first = sem("s_first")
        s_load = sem("s_load")
        s_wtok = sem("s_wtok")
        s_setup_pool = sem("s_setup_pool")
        s_setup_pe = sem("s_setup_pe")
        s_setup_act = sem("s_setup_act")
        s_setup_dve = sem("s_setup_dve")
        pe_done, act_done, dve_done, pool_done = (sem(f"{n}_done") for n in ("pe", "act", "dve", "pool"))
        s_release = sem("s_release")
        r_pe, r_act, r_dve, s_wkv, s_x = (sem(n) for n in ("r_pe", "r_act", "r_dve", "s_wkv", "s_x"))
        s_adding = [sem(f"s_adding{l}") for l in range(2)]
        s_top = [sem(f"s_top{l}") for l in range(2)]
        m_pe, m_act, m_dve, m_pool = (sem(n) for n in ("m_pe", "m_act", "m_dve", "m_pool"))
        f_pe, f_act, f_dve, f_pool = ([sem(f"f{l}_{n}") for l in range(2)] for n in ("pe", "act", "dve", "pool"))
        s_bcw = sem("s_bcw")
        s_bcb = [sem(f"s_bcb{k}") for k in range(3)]
        s_wew = [sem(f"s_wew{l}") for l in range(2)]
        s_wb = [[sem(f"s_wb{l}_{k}") for k in range(2)] for l in range(2)]
        s_out = sem("s_out")
        block = ctx.enter_context(nc.Block())

        def pipeline(eng, iteration):
            last = NCH + STAGES - 1
            full = (STAGES - 1, NCH)
            for i in range(full[0]):
                iteration(i, [s for s in range(STAGES) if 0 <= i - s < NCH])
            with eng.Fori(*full) as i:
                iteration(i, list(range(STAGES)))
            for i in range(full[1], last):
                iteration(i, [s for s in range(STAGES) if 0 <= i - s < NCH])

        def meet(eng, done, i):
            eng.drain().then_inc(done, 1)
            eng.wait_ge(s_release, i + 1)

        def layers(on):
            return [(l, s) for l, s in enumerate(FFN) if s in on]

        def blocks(on):
            return [(l, s, k) for half in range(HB // 2) for l, s in layers(on) for k in (2 * half, 2 * half + 1)]

        first_loads = [
            (Wk[:], a["Wk"]), (Wv[:], a["Wv"]), (Wr[:], a["Wr"]), (Wcr[:], a["Wcr"]), (Wck[:], a["Wck"]),
            (Wcv[:], a["Wcv"].rearrange("(k p) c -> p k c", p=P)),
            *[(cols[:, k:k + 1], a[n]) for n, k in (("time_decay", W_COL), ("time_first", U_COL), ("ts", TS_COL),
              ("ln1_g", G1), ("ln1_b", B1), ("ln2_g", G2), ("ln2_b", B2))],
        ]
        loads = [
            (Aneg[:], a["A_log"].rearrange("(h p) n -> p h n", p=P)),
            (gate[:], a["output_gate"].partition_broadcast(P)),
            (rw1[:], a["rw1"]),
            (rw2[:], a["rw2"].rearrange("(k p) e -> p k e", p=P)),
            (rb2[:], a["rb2"].partition_broadcast(P)),
            (w1[:], a["w1"].rearrange("e c h -> c e h")),
            (w2[:], a["w2"].rearrange("e (k p) c -> p e k c", p=P)),
        ]
        element_loads = [
            (bdt[:], a["b_dt"].rearrange("(h p) -> p h", p=P)),
            (Dp[:], a["D"].rearrange("(h p) -> p h", p=P)),
            (rb1[:], a["rb1"].rearrange("(k p) -> p k", p=P)),
            *[(b1[:, e, :], a["b1"][e].rearrange("(k p) -> p k", p=P)) for e in range(E)],
            (b2[:], a["b2"].rearrange("e c -> c e")),
        ]
        win_tok = sz[:].rearrange("p h (k c) -> p (h k) c", c=C)[:, 0:4, :]
        wdt_tok = hid[0][:, 0:DH, 0:DI]
        wbc_tok = hid[1][0:2 * NS, 0, 0:DI]
        wout_tok = hid[1][:, 1, 0:DI]
        tok_loads = [
            (win_tok, a["W_in"].rearrange("(k p) c -> p k c", p=P)),
            (wdt_tok, a["W_dt"].rearrange("(h p) d -> p h d", p=P)),
            (wbc_tok[0:NS], a["W_B"]), (wbc_tok[NS:2 * NS], a["W_C"]),
            (wout_tok, a["W_out"]),
        ]
        n_first = 16 * len(first_loads)
        n_load, n_tok = 16 * (len(loads) + len(element_loads)), 16 * len(tok_loads)

        @block.sync
        def _(sp):
            for dst, src in first_loads:
                sp.dma_start(dst, src).then_inc(s_first, 16)

            def iteration(i, on):
                c = {s: i - s for s in on}
                if RWKV in on:
                    sp.dma_start(xtok[:], a["x"][:, bass.ds(i, 1), :, :].rearrange("b o t c -> t (o b) c")
                                 ).then_inc(s_x, 16)
                if on == FIRST:
                    for dst, src in tok_loads:
                        sp.dma_start(dst, src).then_inc(s_wtok, 16)
                    for dst, src in loads:
                        sp.dma_start(dst, src).then_inc(s_load, 16)
                    for dst, src in element_loads:
                        sp.dma_start(dst, src, allow_slow_non_contiguous=True).then_inc(s_load, 16)

                def bc_rows(k):
                    q, part = divmod(k, 2)
                    sp.dma_start(bcb[:, k % 3], bc_dram[part, q * NG:(q + 1) * NG, :].partition_broadcast(P)
                                 ).then_inc(s_bcb[k % 3], 16)

                def we_row(l, e):
                    sp.dma_start(wb[l][:, e % 2, :], we_dram[l][e].partition_broadcast(P)
                                 ).then_inc(s_wb[l][e % 2], 16)

                if MAMBA in on:
                    sp.wait_ge(m_act, at(c[MAMBA], M_ACT, "bc"))
                    sp.dma_start(bc_dram.rearrange("k n t -> (k n) t"), bcs).then_inc(s_bcw, 16)
                    sp.wait_ge(s_bcw, loads_by(c[MAMBA], 1, 1))
                    for k in range(3):
                        bc_rows(k)
                for l, _ in layers(on):
                    sp.wait_ge(f_act[l], at(c[FFN[l]], F_ACT[l], "weT"))
                    sp.dma_start(we_dram[l], weT[l]).then_inc(s_wew[l], 16)
                for l, _ in layers(on):
                    sp.wait_ge(s_wew[l], loads_by(c[FFN[l]], 1, 1))
                    we_row(l, 0)
                    we_row(l, 1)
                for j in range(E):
                    if MAMBA in on and j % 2:
                        for k, used in ((j + 2, f"bu{j}"), (j + 3, f"hc{j}")):
                            if k < 2 * Q:
                                sp.wait_ge(m_pool, at(c[MAMBA], M_POOL, used))
                                bc_rows(k)
                    if j + 2 < E:
                        for l, _ in layers(on):
                            sp.wait_ge(f_dve[l], at(c[FFN[l]], F_DVE[l], f"t{j}"))
                            we_row(l, j + 2)
                if FFN1 in on:
                    sp.wait_ge(f_act[1], at(c[FFN1], F_ACT[1], "o"))
                    sp.dma_start(out[:, bass.ds(i - FFN1, 1), :, :].rearrange("b o t c -> t (o b) c"), otok[:]
                                 ).then_inc(s_out, 16)
                for done in (pe_done, act_done, dve_done, pool_done):
                    sp.wait_ge(done, i + 1)
                if FFN1 in on:
                    sp.wait_ge(s_out, loads_by(c[FFN1], 1, 1))
                sp.sem_inc(s_release, 1)

            pipeline(sp, iteration)

        @block.gpsimd
        def _(pool):
            g = nc.gpsimd
            g.memset(ident[:], 0.0).then_inc(s_setup_pool, 1)
            pool.wait_ge(s_setup_pool, 1)
            g.affine_select(out=ident[:], in_=ident[:], compare_op=ALU.not_equal, fill=1.0, base=0,
                            pattern=[[-1, P]], channel_multiplier=1).then_inc(s_setup_pool, 1)
            g.iota(iota_i[:], pattern=[[1, E]], base=0, channel_multiplier=0).then_inc(s_setup_pool, 1)
            g.memset(ones_mean[:], 1.0 / C).then_inc(s_setup_pool, 1)
            g.memset(eps[:], EPS).then_inc(s_setup_pool, 1)
            pool.wait_ge(s_setup_pool, 5)
            g.tensor_tensor(centre[:], ident[:], ones_mean[:], ALU.subtract).then_inc(s_setup_pool, 1)
            g.memset(abuf[:], 0.0).then_inc(s_setup_pool, 1)
            g.memset(hst[:], 0.0).then_inc(s_setup_pool, 1)
            pool.wait_ge(s_setup_pool, 8)

            def iteration(i, on):
                c = {s: i - s for s in on}
                def scan_operand(j):
                    q, h = divmod(j, DH)
                    if j >= DH:
                        pool.wait_ge(m_dve, at(c[MAMBA], M_DVE, f"save{j - DH}"))
                        pool.wait_ge(m_pool, at(c[MAMBA], M_POOL, f"hc{j - DH}"))
                    if h == 0:
                        pool.wait_ge(s_bcb[2 * q % 3], rows_in(c[MAMBA], 2 * q))
                    pool.wait_ge(m_dve, at(c[MAMBA], M_DVE, f"u{h}"))
                    g.tensor_tensor(bbuf[:, h, :, :, 1:], du[:, h].unsqueeze(1).to_broadcast([P, NG, B, TC]),
                                    bcb[:, 2 * q % 3].rearrange("p n (b t) -> p n b t", b=B), ALU.mult
                                    ).then_inc(m_pool, 1)
                    g.tensor_copy(bbuf[:, h, :, :, 0], hst[:, j]).then_inc(m_pool, 1)

                def add_expert(e):
                    for l, s in layers(on):
                        pool.wait_ge(f_dve[l], at(c[FFN[l]], F_DVE[l], f"t{e}"))
                        if e:
                            pool.wait_ge(f_pool[l], at(c[FFN[l]], F_POOL[l], f"acc{e - 1}"))
                        pool.sem_inc(s_adding[l], 1)
                        acc = X[:, bass.ds(i - s, 1), :].squeeze(1)
                        g.tensor_tensor(acc, acc, t1[l][:], ALU.add).then_inc(f_pool[l], 1)

                if MAMBA in on:
                    scan_operand(0)
                for j in range(E):
                    if MAMBA in on and j + 1 < UNITS:
                        scan_operand(j + 1)
                    if j:
                        add_expert(j - 1)
                    if MAMBA in on:
                        q, h = divmod(j, DH)
                        if h == 0:
                            pool.wait_ge(s_bcb[(2 * q + 1) % 3], rows_in(c[MAMBA], 2 * q + 1))
                        pool.wait_ge(m_dve, at(c[MAMBA], M_DVE, f"scan{j}"))
                        g.tensor_tensor(abuf[:, h, :, :, 1:], bbuf[:, h, :, :, 1:],
                                        bcb[:, (2 * q + 1) % 3].rearrange("p n (b t) -> p n b t", b=B), ALU.mult
                                        ).then_inc(m_pool, 1)
                        if j in PAIRED:
                            pool.wait_ge(m_pool, at(c[MAMBA], M_POOL, f"hc{j}"))
                            g.tensor_tensor(abuf[:, h, 0:2, :, 1:], abuf[:, h, 0:2, :, 1:], abuf[:, h, 2:4, :, 1:],
                                            ALU.add).then_inc(m_pool, 1)
                add_expert(E - 1)
                meet(pool, pool_done, i)

            pipeline(pool, iteration)

        @block.tensor
        def _(pe):
            mm = nc.tensor.matmul

            pe.wait_ge(s_setup_pool, 6)
            pe.wait_ge(s_first, n_first)

            def transpose_weights():
                pe.wait_ge(s_wtok, n_tok)
                for k in range(4):
                    last = nc.tensor.transpose(H0[:, k * P:(k + 1) * P], win_tok[:, k, :], ident[:])
                last.then_inc(s_setup_pe, 1)
                for h in range(DH):
                    for o in range(DH):
                        last = nc.tensor.transpose(H1[:, h * DI + o * P:h * DI + (o + 1) * P],
                                                   wdt_tok[:, o, h * P:(h + 1) * P], ident[:])
                last.then_inc(s_setup_pe, 1)
                for h in range(DH):
                    last = nc.tensor.transpose(M0[:, h * 2 * NS:(h + 1) * 2 * NS],
                                               wbc_tok[:, h * P:(h + 1) * P], ident[0:2 * NS, 0:2 * NS])
                last.then_inc(s_setup_pe, 1)
                for h in range(DH):
                    last = nc.tensor.transpose(M1[:, h * C:(h + 1) * C], wout_tok[:, h * P:(h + 1) * P], ident[:])
                last.then_inc(s_setup_pe, 1)
                pe.wait_ge(s_load, n_load)

            def iteration(i, on):
                c = {s: i - s for s in on}
                R, M = RWKV in on, MAMBA in on
                chunk = {s: X[:, bass.ds(c[s], 1), :].squeeze(1) for s in on}

                def less_mean(ps, src, s):
                    mm(ps[:], centre[:], src, start=True, stop=True).then_inc(s, 1)

                def average(ps, src, s):
                    mm(ps[:], ones_mean[:], src, start=True, stop=True).then_inc(s, 1)

                if M:
                    less_mean(M0, chunk[MAMBA], m_pe)
                for l, s in layers(on):
                    less_mean(OB[l], chunk[s], f_pe[l])
                if M:
                    pe.wait_ge(m_act, at(c[MAMBA], M_ACT, "sq"))
                    average(M1, sq_m, m_pe)
                for l, s in layers(on):
                    pe.wait_ge(f_act[l], at(c[FFN[l]], F_ACT[l], "sq"))
                    average(HV[l], hid[l][:, 0, :], f_pe[l])
                def router(l):
                    pe.wait_ge(f_dve[l], at(c[FFN[l]], F_DVE[l], "xn"))
                    if l == 0 and FFN1 in on:
                        pe.wait_ge(f_act[1], at(c[FFN1], F_ACT[1], "ln"))
                    for k in range(HB):
                        if k >= 2:
                            pe.wait_ge(f_act[l], at(c[FFN[l]], F_ACT[l], f"sr{k - 2}"))
                        elif l and FFN0 in on:
                            pe.wait_ge(f_act[0], at(c[FFN0], F_ACT[0], f"sr{k + 2}"))
                        mm((H0, H1)[k % 2][:], rw1[:, k * P:(k + 1) * P], xf[l][:], start=True, stop=True
                           ).then_inc(f_pe[l], 1)

                def logits(l):
                    pe.wait_ge(f_act[l], at(c[FFN[l]], F_ACT[l], "sr3"))
                    for b in range(B):
                        for k in range(HB):
                            last = mm(OB[l][:, b * E:(b + 1) * E], hid[l][:, k, b * TC:(b + 1) * TC], rw2[:, k, :],
                                      start=(k == 0), stop=(k == HB - 1))
                    last.then_inc(f_pe[l], 1)

                if R:
                    pe.wait_ge(s_x, loads_by(c[RWKV], 1, 1))
                    for b in range(B):
                        last = nc.tensor.transpose(A0[:, b * TC:(b + 1) * TC], xtok[:, b, :], ident[:])
                    last.then_inc(r_pe, 1)
                    pe.wait_ge(r_act, at(c[RWKV], R_ACT, "xin"))
                    less_mean(A1, xin[:], r_pe)
                if M:
                    pe.wait_ge(m_dve, at(c[MAMBA], M_DVE, "xn"))
                    mm(M1[:], WinT[:, 0:P], rs_m[:], start=True, stop=True).then_inc(m_pe, 1)
                    mm(M0[:], WinT[:, P:2 * P], rs_m[:], start=True, stop=True).then_inc(m_pe, 1)
                if R:
                    pe.wait_ge(r_act, at(c[RWKV], R_ACT, "sq0"))
                    average(A0, sq_r[:], r_pe)
                if M:
                    pe.wait_ge(m_act, at(c[MAMBA], M_ACT, "xs1"))
                    for h in range(DH):
                        last = mm(M1[0:2 * NS, :], WbcT[:, h, :], xs[:, h], start=(h == 0), stop=(h == DH - 1))
                    last.then_inc(m_pe, 1)
                if M:
                    for o, ps in ((0, M0), (1, M1)):
                        if o:
                            pe.wait_ge(m_act, at(c[MAMBA], M_ACT, "bc"))
                        for h in range(DH):
                            last = mm(ps[:], WdtT[:, h, o * P:(o + 1) * P], xs[:, h],
                                      start=(h == 0), stop=(h == DH - 1))
                        last.then_inc(m_pe, 1)
                if M:
                    for h, ps in ((0, M0), (1, M1)):
                        pe.wait_ge(m_act, at(c[MAMBA], M_ACT, f"mx{h}"))
                        mm(ps[:], WinT[:, (DH + h) * P:(DH + h + 1) * P], rs_m[:], start=True, stop=True
                           ).then_inc(m_pe, 1)
                if R:
                    pe.wait_ge(r_act, at(c[RWKV], R_ACT, "h"))
                    mm(A1[:], Wk[:], hs1[:, :, 0:TC], start=True, stop=True).then_inc(r_pe, 1)
                    mm(A0[:], Wv[:], hs1[:, :, 0:TC], start=True, stop=True).then_inc(r_pe, 1)
                if FFN0 in on:
                    router(0)
                if FFN1 in on:
                    router(1)
                if R:
                    pe.wait_ge(r_act, at(c[RWKV], R_ACT, "k"))
                    mm(A1[:], Wr[:], hs1[:, :, 0:TC], start=True, stop=True).then_inc(r_pe, 1)
                if on == FIRST:
                    transpose_weights()
                for l, s in layers(on):
                    logits(l)

                def weights_to_rows(l):
                    pe.wait_ge(f_dve[l], at(c[FFN[l]], F_DVE[l], "we"))
                    for b in range(B):
                        last = nc.tensor.transpose(OB[l][0:E, b * TC:(b + 1) * TC], we[l][:, b, :], ident[:])
                    last.then_inc(f_pe[l], 1)

                def second_norm_centre():
                    pe.wait_ge(r_act, at(c[RWKV], R_ACT, "tr"))
                    pe.wait_ge(r_dve, at(c[RWKV], R_DVE, "x1"))
                    less_mean(A0, x0[:], r_pe)

                def second_norm_variance():
                    pe.wait_ge(r_act, at(c[RWKV], R_ACT, "sq2"))
                    average(A1, sq_r[:], r_pe)

                if M:
                    pe.wait_ge(m_act, at(c[MAMBA], M_ACT, "sz1"))
                for e in range(E):
                    for l, s, k in blocks(on):
                        if k >= 2:
                            pe.wait_ge(f_act[l], at(c[FFN[l]], F_ACT[l], f"h{e}_{k - 2}"))
                        elif e:
                            pe.wait_ge(f_act[l], at(c[FFN[l]], F_ACT[l], f"h{e - 1}_{k + 2}"))
                        mm(HR[l][k % 2][:], w1[:, e, k * P:(k + 1) * P], xf[l][:], start=True, stop=True
                           ).then_inc(f_pe[l], 1)
                    if e == 0:
                        for l, s in layers(on):
                            weights_to_rows(l)
                    if R and e == E - 1 and layers(on):
                        second_norm_centre()
                    for l, s in layers(on):
                        if e:
                            pe.wait_ge(f_dve[l], at(c[FFN[l]], F_DVE[l], f"t{e - 1}"))
                        else:
                            pe.wait_ge(f_act[l], at(c[FFN[l]], F_ACT[l], "weT"))
                        for k in range(HB):
                            pe.wait_ge(f_act[l], at(c[FFN[l]], F_ACT[l], f"h{e}_{k}"))
                            last = mm(OB[l][:], w2[:, e, k, :], hid[l][:, k, :], start=(k == 0), stop=(k == HB - 1))
                        last.then_inc(f_pe[l], 1)
                        if R and e == E - 1 and l == layers(on)[0][0]:
                            second_norm_variance()
                if R:
                    if not layers(on):
                        second_norm_centre()
                        second_norm_variance()
                    pe.wait_ge(r_act, at(c[RWKV], R_ACT, "h2"))
                    for k in range(HB):
                        mm(CK[k][:], Wck[:, k * P:(k + 1) * P], hs2[:, :, 0:TC], start=True, stop=True
                           ).then_inc(r_pe, 1)
                if R:
                    mm(H1[:], Wcr[:], hs2[:, :, 0:TC], start=True, stop=True).then_inc(r_pe, 1)
                    for k in range(HB):
                        pe.wait_ge(r_act, at(c[RWKV], R_ACT, f"kk{k}"))
                        last = mm(A1[:], Wcv[:, k, :], kk[:, k, :], start=(k == 0), stop=(k == HB - 1))
                    last.then_inc(r_pe, 1)
                if FFN1 in on:
                    pe.wait_ge(f_act[1], at(c[FFN1], F_ACT[1], "xo"))
                    for b in range(B):
                        last = nc.tensor.transpose(H0[:, b * C:(b + 1) * C], xo[:, b * TC:(b + 1) * TC], ident[:])
                    last.then_inc(f_pe[1], 1)
                if M:
                    for h in range(DH):
                        pe.wait_ge(m_dve, at(c[MAMBA], M_DVE, f"yz{h}"))
                        last = mm(M0[:], WoutT[:, h, :], ya[:, h, :], start=(h == 0), stop=(h == DH - 1))
                    last.then_inc(m_pe, 1)
                meet(pe, pe_done, i)

            pipeline(pe, iteration)

        @block.scalar
        def _(act):
            f = nc.scalar.activation

            nc.scalar.preload_act_table_set(STATS)
            act.wait_ge(s_first, n_first)
            f(cols[:, EU:EU + 1], cols[:, U_COL:U_COL + 1], ACT.Exp).then_inc(s_setup_act, 1)
            act.wait_ge(s_setup_pool, 5)

            def keep_weights():
                act.wait_ge(s_setup_pe, 4)
                nc.scalar.copy(WinT[:], H0[:]).then_inc(s_setup_act, 1)
                nc.scalar.copy(WdtT[:].rearrange("p h d -> p (h d)"), H1[:]).then_inc(s_setup_act, 1)
                nc.scalar.copy(WbcT[:].rearrange("p h n -> p (h n)"), M0[:, 0:DH * 2 * NS]).then_inc(s_setup_act, 1)
                nc.scalar.copy(WoutT[:].rearrange("p h c -> p (h c)"), M1[:, 0:DH * C]).then_inc(s_setup_act, 1)
                nc.scalar.preload_act_table_set(STATS)
                act.wait_ge(s_load, n_load)
                f(Aneg[:], Aneg[:], ACT.Exp).then_inc(s_setup_act, 1)
                f(gate[:], gate[:], ACT.Exp, scale=-1.0).then_inc(s_setup_act, 1)

            def iteration(i, on):
                c = {s: i - s for s in on}
                R, M = RWKV in on, MAMBA in on

                def router(l):
                    for k in range(HB):
                        act.wait_ge(f_pe[l], at(c[FFN[l]], F_PE[l], f"r{k}"))
                        f(hid[l][:, k, :], (H0, H1)[k % 2][:], ACT.Silu, bias=rb1[:, k:k + 1]).then_inc(f_act[l], 1)

                def rstd(var, dst, s, done, ln, chunk):
                    f(dst, var, ACT.Ln, bias=eps[:]).then_inc(s, 1)
                    act.wait_ge(s, at(chunk, done, ln))
                    f(dst, dst, ACT.Exp, scale=-0.5).then_inc(s, 1)

                if M:
                    act.wait_ge(m_pe, at(c[MAMBA], M_PE, "cen"))
                    f(sq_m, M0[:], ACT.Square).then_inc(m_act, 1)
                for l, s in layers(on):
                    act.wait_ge(f_pe[l], at(c[FFN[l]], F_PE[l], "cen"))
                    f(hid[l][:, 0, :], OB[l][:], ACT.Square).then_inc(f_act[l], 1)
                if M:
                    act.wait_ge(m_pe, at(c[MAMBA], M_PE, "var"))
                    rstd(M1[:], rs_m[:], m_act, M_ACT, "ln", c[MAMBA])
                if R:
                    act.wait_ge(r_pe, at(c[RWKV], R_PE, "xT"))
                    nc.scalar.copy(xin[:], A0[:]).then_inc(r_act, 1)
                for l, s in layers(on):
                    act.wait_ge(f_pe[l], at(c[FFN[l]], F_PE[l], "var"))
                    rstd(HV[l][:], t1[l][:], f_act[l], F_ACT[l], "ln", c[s])
                if R:
                    act.wait_ge(r_pe, at(c[RWKV], R_PE, "cen0"))
                    f(sq_r[:], A1[:], ACT.Square).then_inc(r_act, 1)
                if M:
                    for h, ps in ((0, M1), (1, M0)):
                        act.wait_ge(m_pe, at(c[MAMBA], M_PE, f"xs{h}"))
                        nc.scalar.copy(xs[:, h].rearrange("p b t -> p (b t)"), ps[:]).then_inc(m_act, 1)
                if R:
                    act.wait_ge(r_pe, at(c[RWKV], R_PE, "var0"))
                    rstd(A0[:], rs_r[:], r_act, R_ACT, "ln0", c[RWKV])
                if M:
                    act.wait_ge(m_pe, at(c[MAMBA], M_PE, "bc"))
                    nc.scalar.copy(bcs, M1[0:2 * NS, :]).then_inc(m_act, 1)
                if M:
                    for h, ps in ((0, M0), (1, M1)):
                        act.wait_ge(m_pe, at(c[MAMBA], M_PE, f"dt{h}"))
                        f(dt[:, h, :], ps[:], ACT.Abs, bias=bdt[:, h:h + 1]).then_inc(m_act, 1)
                        f(mx[h], ps[:].rearrange("p (b t) -> p b t", b=B), ACT.Relu, bias=bdt[:, h:h + 1]
                          ).then_inc(m_act, 1)
                if R:
                    act.wait_ge(r_dve, at(c[RWKV], R_DVE, "var1"))
                    rstd(sq_r[:], rs_r[:], r_act, R_ACT, "ln1", c[RWKV])
                if M:
                    for h in range(DH):
                        act.wait_ge(m_act, at(c[MAMBA], M_ACT, f"ab{h}"))
                        f(dt[:, h, :], dt[:, h, :], ACT.Exp, scale=-1.0).then_inc(m_act, 1)
                if R:
                    act.wait_ge(r_dve, at(c[RWKV], R_DVE, "xn1"))
                    f(hs1[:, :, 1:], xc_r[:].rearrange("p (b t) -> p b t", b=B), ACT.Identity,
                      bias=cols[:, B1:B1 + 1], scale=cols[:, G1:G1 + 1]).then_inc(r_act, 1)
                if M:
                    for h in range(DH):
                        act.wait_ge(m_act, at(c[MAMBA], M_ACT, f"ex{h}"))
                        f(ya[:, h, :], dt[:, h, :], ACT.Ln, bias=1.0).then_inc(m_act, 1)
                if R:
                    act.wait_ge(r_pe, at(c[RWKV], R_PE, "k"))
                    nc.scalar.copy(kb[:, :, 1:], A1[:].rearrange("p (b t) -> p b t", b=B)).then_inc(r_act, 1)
                    act.wait_ge(r_pe, at(c[RWKV], R_PE, "v"))
                    nc.scalar.copy(vb[:].rearrange("p b t -> p (b t)"), A0[:]).then_inc(r_act, 1)
                    act.wait_ge(r_dve, at(c[RWKV], R_DVE, "dkc"))
                    f(gam[:], gam[:], ACT.Exp).then_inc(r_act, 1)
                nc.scalar.preload_act_table_set(SILU)
                if FFN0 in on:
                    router(0)
                if M:
                    for h, ps in ((0, M0), (1, M1)):
                        act.wait_ge(m_pe, at(c[MAMBA], M_PE, f"z{h}"))
                        f(sz[:, h, :], ps[:], ACT.Silu).then_inc(m_act, 1)
                if FFN1 in on:
                    router(1)
                nc.scalar.preload_act_table_set(STATS)

                def decays(j):
                    q, h = divmod(j, DH)
                    if j:
                        nc.scalar.preload_act_table_set(STATS)
                    act.wait_ge(m_dve, at(c[MAMBA], M_DVE, f"dt{h}" if j < DH else f"red{j - DH}"))
                    for n in range(NG):
                        f(abuf[:, h, n, :, 1:], dt[:, h, :].rearrange("p (b t) -> p b t", b=B), ACT.Exp,
                          scale=Aneg[:, h, q * NG + n:q * NG + n + 1]).then_inc(m_act, 1)

                if M:
                    decays(0)
                for l, s in layers(on):
                    act.wait_ge(f_dve[l], at(c[FFN[l]], F_DVE[l], "d"))
                    f(gp[l][:, 1, :], gp[l][:, 0, :], ACT.Exp).then_inc(f_act[l], 1)
                for e in range(E):
                    if layers(on):
                        nc.scalar.preload_act_table_set(SILU)
                    for l, s, k in blocks(on):
                        if e == k == 0:
                            act.wait_ge(f_pe[l], at(c[FFN[l]], F_PE[l], "logits"))
                        act.wait_ge(f_pe[l], at(c[FFN[l]], F_PE[l], f"h{e}_{k}"))
                        f(hid[l][:, k, :], HR[l][k % 2][:], ACT.Silu, bias=b1[:, e, k:k + 1]).then_inc(f_act[l], 1)
                    if e == 0:
                        for l, s in layers(on):
                            act.wait_ge(f_pe[l], at(c[FFN[l]], F_PE[l], "weT"))
                            nc.scalar.copy(weT[l], OB[l][0:E, :]).then_inc(f_act[l], 1)
                        if R:
                            if not layers(on):
                                nc.scalar.preload_act_table_set(SILU)
                            act.wait_ge(r_pe, at(c[RWKV], R_PE, "r"))
                            f(tr[:], A1[:], ACT.Tanh, scale=0.5).then_inc(r_act, 1)
                        if on == FIRST:
                            keep_weights()
                    if M and e + 1 < UNITS:
                        decays(e + 1)
                if R:
                    act.wait_ge(r_pe, at(c[RWKV], R_PE, "cen2"))
                    f(sq_r[:], A0[:], ACT.Square).then_inc(r_act, 1)
                    nc.scalar.preload_act_table_set(STATS)
                    act.wait_ge(r_pe, at(c[RWKV], R_PE, "var2"))
                    rstd(A1[:], rs_r[:], r_act, R_ACT, "ln2", c[RWKV])
                    nc.scalar.preload_act_table_set(SILU)
                    act.wait_ge(r_dve, at(c[RWKV], R_DVE, "xn2"))
                    f(hs2[:, :, 1:], xc_r[:].rearrange("p (b t) -> p b t", b=B), ACT.Identity,
                      bias=cols[:, B2:B2 + 1], scale=cols[:, G2:G2 + 1]).then_inc(r_act, 1)
                    if M:
                        act.wait_ge(m_dve, at(c[MAMBA], M_DVE, f"save{UNITS - DH}"))
                        act.wait_ge(m_pool, at(c[MAMBA], M_POOL, f"hc{UNITS - DH}"))
                    for k in range(HB):
                        act.wait_ge(r_pe, at(c[RWKV], R_PE, f"ck{k}"))
                        f(kk[:, k, :], CK[k][:], ACT.Relu).then_inc(r_act, 1)
                        act.wait_ge(r_act, at(c[RWKV], R_ACT, f"relu{k}"))
                        f(kk[:, k, :], kk[:, k, :], ACT.Square).then_inc(r_act, 1)
                if R:
                    act.wait_ge(r_pe, at(c[RWKV], R_PE, "cr"))
                    f(tr[:], H1[:], ACT.Tanh, scale=0.5).then_inc(r_act, 1)
                if FFN1 in on:
                    act.wait_ge(f_pool[1], at(c[FFN1], F_POOL[1], f"acc{E - 1}"))
                    nc.scalar.copy(xo[:], X[:, bass.ds(i - FFN1, 1), :].squeeze(1)).then_inc(f_act[1], 1)
                    act.wait_ge(f_pe[1], at(c[FFN1], F_PE[1], "oT"))
                    nc.scalar.copy(otok[:].rearrange("p b c -> p (b c)"), H0[:]).then_inc(f_act[1], 1)
                nc.scalar.preload_act_table_set(STATS)
                meet(act, act_done, i)

            pipeline(act, iteration)

        @block.vector
        def _(dve):
            v = nc.vector
            tt, stt, ts = v.tensor_tensor, v.scalar_tensor_tensor, v.tensor_scalar

            dve.wait_ge(s_first, n_first)
            ts_col = cols[:, TS_COL:TS_COL + 1].unsqueeze(1).to_broadcast([P, B, 1])
            v.tensor_copy(hs1[:, :, TC:], ts_col).then_inc(s_setup_dve, 1)
            v.tensor_copy(hs2[:, :, TC:], ts_col).then_inc(s_setup_dve, 1)
            v.memset(kb[:, :, TC:], -1e4).then_inc(s_setup_dve, 1)
            v.memset(aab[:, :, TC:], 0.0).then_inc(s_setup_dve, 1)
            v.memset(pb[:, :, TC:], 0.0).then_inc(s_setup_dve, 1)
            v.memset(cb[:, :, TC:], 1.0).then_inc(s_setup_dve, 1)
            dve.wait_ge(s_setup_dve, 6)
            dve.wait_ge(s_setup_act, 1)

            def finish_weights():
                dve.wait_ge(s_setup_act, 7)
                ts(gate[:], gate[:], 1.0, None, ALU.add).then_inc(s_setup_dve, 1)
                ts(Aneg[:], Aneg[:], -1.0, None, ALU.mult).then_inc(s_setup_dve, 1)
                dve.wait_ge(s_setup_dve, 7)
                v.reciprocal(gate[:], gate[:]).then_inc(s_setup_dve, 1)
                dve.wait_ge(s_setup_pool, 8)
                v.tensor_copy(iota_f[:], iota_i[:]).then_inc(s_setup_dve, 1)
                dve.wait_ge(s_load, n_load)

            def iteration(i, on):
                c = {s: i - s for s in on}
                R, M = RWKV in on, MAMBA in on
                chunk = {s: X[:, bass.ds(c[s], 1), :].squeeze(1) for s in on}

                def gates_1(l):
                    dve.wait_ge(f_pe[l], at(c[FFN[l]], F_PE[l], "logits"))
                    tt(lg[l][:], OB[l][:, 0:B * E].rearrange("p (b e) -> p b e", b=B),
                       rb2[:].unsqueeze(1).to_broadcast([P, B, E]), ALU.add).then_inc(s_top[l], 1)
                    dve.wait_ge(s_top[l], 1)
                    for b in range(B):
                        v.max(top[l][:, b, :], lg[l][:, b, :]).then_inc(s_top[l], 1)
                    for b in range(B):
                        dve.wait_ge(s_top[l], 2 + b)
                        v.max_index(idx[l][:, b, :], top[l][:, b, :], lg[l][:, b, :]).then_inc(s_top[l], 1)
                    dve.wait_ge(s_top[l], 1 + 2 * B)
                    v.tensor_copy(idf[l][:], idx[l][:]).then_inc(f_dve[l], 1)
                    tt(gp[l][:, 0, :], top[l][:, :, 1], top[l][:, :, 0], ALU.subtract).then_inc(f_dve[l], 1)

                def gates_2(l):
                    g = gp[l]
                    dve.wait_ge(f_act[l], at(c[FFN[l]], F_ACT[l], "gex"))
                    ts(g[:, 2, :], g[:, 1, :], 1.0, None, ALU.add).then_inc(f_dve[l], 1)
                    dve.wait_ge(f_dve[l], at(c[FFN[l]], F_DVE[l], "den"))
                    v.reciprocal(g[:, 3, :], g[:, 2, :]).then_inc(f_dve[l], 1)
                    dve.wait_ge(f_dve[l], at(c[FFN[l]], F_DVE[l], "p0"))
                    tt(g[:, 4, :], g[:, 1, :], g[:, 3, :], ALU.mult).then_inc(f_dve[l], 1)
                    for k in range(TOPK):
                        m = mk[l][:, k]
                        tt(m, iota_f[:].unsqueeze(1).to_broadcast([P, B, E]),
                           idf[l][:, :, k:k + 1].to_broadcast([P, B, E]), ALU.is_equal).then_inc(f_dve[l], 1)
                        dve.wait_ge(f_dve[l], at(c[FFN[l]], F_DVE[l], f"m{k}"))
                        tt(m, m, g[:, 3 + k, :].unsqueeze(2).to_broadcast([P, B, E]), ALU.mult).then_inc(f_dve[l], 1)
                    dve.wait_ge(f_dve[l], at(c[FFN[l]], F_DVE[l], "w1"))
                    tt(we[l], mk[l][:, 0], mk[l][:, 1], ALU.add).then_inc(f_dve[l], 1)

                def wkv_step(t):
                    r, p, c = rb[:, :, t], pb[:, :, t], cb[:, :, t]
                    bb = bbs[:, t % 2]
                    if t:
                        dve.wait_ge(s_wkv, 5 * t - 1)
                    stt(out=r, in0=p, scalar=1.0, in1=gam[:, :, t], op0=ALU.add, op1=ALU.mult).then_inc(s_wkv, 1)
                    if t:
                        dve.wait_ge(s_wkv, 5 * t)
                    stt(out=bb, in0=p, scalar=1.0, in1=c, op0=ALU.add, op1=ALU.mult).then_inc(s_wkv, 1)
                    dve.wait_ge(s_wkv, 5 * t + 1)
                    v.reciprocal(rcp[:], r).then_inc(s_wkv, 1)
                    dve.wait_ge(s_wkv, 5 * t + 2)
                    stt(out=pb[:, :, t + 1], in0=r, scalar=R_MAX, in1=bb, op0=ALU.min, op1=ALU.mult).then_inc(s_wkv, 1)
                    dve.wait_ge(s_wkv, 5 * t + 3)
                    ts(cb[:, :, t + 1], rcp[:], 1.0, 1.0 / R_MAX, ALU.min, ALU.max).then_inc(s_wkv, 1)

                num, den = sq_r[:].rearrange("p (b t) -> p b t", b=B), rs_r[:].rearrange("p (b t) -> p b t", b=B)
                rm = kb[:, :, 0:TC]
                eu = cols[:, EU:EU + 1]

                def scan(j):
                    h = j % DH
                    dve.wait_ge(m_act, at(c[MAMBA], M_ACT, f"exp{j}_{NG - 1}"))
                    dve.wait_ge(m_pool, at(c[MAMBA], M_POOL, f"edge{j}"))
                    flat = [x[:, h].rearrange("p n b t -> p (n b t)") for x in (abuf, bbuf)]
                    v.tensor_tensor_scan(flat[1], flat[0], flat[1], 0.0, ALU.mult, ALU.add).then_inc(m_dve, 1)
                    dve.wait_ge(m_dve, at(c[MAMBA], M_DVE, f"scan{j}"))
                    v.tensor_copy(hst[:, j], bbuf[:, h, :, :, TC]).then_inc(m_dve, 1)

                def state_and_parts():
                    dve.wait_ge(s_wkv, 5 * TC)
                    ts(rm, rb[:], 1.0, None, ALU.min).then_inc(r_dve, 1)
                    tt(gam[:], vb[:], cb[:, :, 1:], ALU.mult).then_inc(r_dve, 1)
                    dve.wait_ge(r_dve, at(c[RWKV], R_DVE, "vc"))
                    for b in range(B):
                        v.tensor_tensor_scan(aab[:, b, 1:], rm[:, b, :], gam[:, b, :], aab[:, b, 0:1],
                                             ALU.mult, ALU.add).then_inc(r_dve, 1)
                    dve.wait_ge(r_dve, at(c[RWKV], R_DVE, "aa3"))
                    stt(out=num, in0=rb[:], scalar=R_MAX, in1=aab[:, :, 0:TC], op0=ALU.min, op1=ALU.mult
                        ).then_inc(r_dve, 1)
                    ts(den, pb[:, :, 1:], eu, None, ALU.add).then_inc(r_dve, 1)

                def fraction():
                    dve.wait_ge(r_dve, at(c[RWKV], R_DVE, "den"))
                    v.reciprocal(den, den).then_inc(r_dve, 1)
                    stt(out=num, in0=vb[:], scalar=eu, in1=num, op0=ALU.mult, op1=ALU.add).then_inc(r_dve, 1)
                    dve.wait_ge(r_dve, at(c[RWKV], R_DVE, "num"))
                    tt(num, num, den, ALU.mult).then_inc(r_dve, 1)
                    dve.wait_ge(r_dve, at(c[RWKV], R_DVE, "y"))
                    dve.wait_ge(r_act, at(c[RWKV], R_ACT, "tr"))
                    stt(out=sq_r[:], in0=tr[:], scalar=1.0, in1=sq_r[:], op0=ALU.add, op1=ALU.mult).then_inc(r_dve, 1)
                    dve.wait_ge(r_dve, at(c[RWKV], R_DVE, "ys"))
                    stt(out=x0[:], in0=sq_r[:], scalar=0.5, in1=x0[:], op0=ALU.mult, op1=ALU.add).then_inc(r_dve, 1)

                def second_norm():
                    dve.wait_ge(r_act, at(c[RWKV], R_ACT, "rstd2"))
                    tt(xc_r[:], A0[:], rs_r[:], ALU.mult).then_inc(r_dve, 1)

                def wkv_steps(part, half=None):
                    first, end = sum(STEPS[:part]), sum(STEPS[:part + 1])
                    middle = (first + end) // 2
                    for t in range(middle if half == 1 else first, middle if half == 0 else end):
                        wkv_step(t)

                if M:
                    dve.wait_ge(m_act, at(c[MAMBA], M_ACT, "rstd"))
                    tt(rs_m[:], M0[:], rs_m[:], ALU.mult).then_inc(m_dve, 1)
                for l, s in layers(on):
                    dve.wait_ge(f_act[l], at(c[s], F_ACT[l], "rstd"))
                    tt(xf[l][:], OB[l][:], t1[l][:], ALU.mult).then_inc(f_dve[l], 1)
                if R:
                    for buf in (hs1, hs2, kb, aab, pb, cb):
                        v.tensor_copy(buf[:, :, 0:1], buf[:, :, TC:]).then_inc(r_dve, 1)
                    dve.wait_ge(r_act, at(c[RWKV], R_ACT, "rstd0"))
                    tt(sq_r[:], A0[:], rs_r[:], ALU.mult).then_inc(r_dve, 1)
                    tt(x0[:], A1[:], rs_r[:], ALU.mult).then_inc(r_dve, 1)
                    dve.wait_ge(r_dve, at(c[RWKV], R_DVE, "vr"))
                    tt(sq_r[:], sq_r[:], rs_r[:], ALU.mult).then_inc(r_dve, 1)
                    dve.wait_ge(r_act, at(c[RWKV], R_ACT, "rstd1"))
                    tt(xc_r[:], x0[:], rs_r[:], ALU.mult).then_inc(r_dve, 1)
                if M:
                    dus = [du[:, h].rearrange("p b t -> p (b t)") for h in range(DH)]
                    for k, coef in enumerate((-4.0 / 3.0, 2.0, -4.0)):
                        for h in range(DH):
                            if k == 0:
                                dve.wait_ge(m_act, at(c[MAMBA], M_ACT, f"ex{h}"))
                            else:
                                dve.wait_ge(m_dve, at(c[MAMBA], M_DVE, f"p{k - 1}{h}"))
                            stt(out=dus[h], in0=dus[h] if k else dt[:, h, :], scalar=coef, in1=dt[:, h, :],
                                op0=ALU.add, op1=ALU.mult).then_inc(m_dve, 1)
                if R:
                    dve.wait_ge(r_act, at(c[RWKV], R_ACT, "k"))
                    stt(out=gam[:], in0=kb[:, :, 0:TC], scalar=cols[:, W_COL:W_COL + 1], in1=kb[:, :, 1:],
                        op0=ALU.add, op1=ALU.subtract).then_inc(r_dve, 1)
                    dve.wait_ge(r_dve, at(c[RWKV], R_DVE, "dk"))
                    ts(gam[:], gam[:], G_MAX, G_MIN, ALU.min, ALU.max).then_inc(r_dve, 1)
                if M:
                    for h in range(DH):
                        dve.wait_ge(m_act, at(c[MAMBA], M_ACT, f"lp{h}"))
                        stt(out=ya[:, h, :], in0=dt[:, h, :], scalar=LN_FROM, in1=ya[:, h, :],
                            op0=ALU.is_ge, op1=ALU.mult).then_inc(m_dve, 1)
                    for h in range(DH):
                        dve.wait_ge(m_dve, at(c[MAMBA], M_DVE, f"g{h}"))
                        stt(out=dus[h], in0=dus[h], scalar=-0.25, in1=ya[:, h, :],
                            op0=ALU.mult, op1=ALU.max).then_inc(m_dve, 1)
                    for h in range(DH):
                        dve.wait_ge(m_dve, at(c[MAMBA], M_DVE, f"lc{h}"))
                        tt(dt[:, h, :].rearrange("p (b t) -> p b t", b=B), du[:, h], mx[h], ALU.add).then_inc(m_dve, 1)
                    for h in range(DH):
                        dve.wait_ge(m_dve, at(c[MAMBA], M_DVE, f"dt{h}"))
                        tt(dus[h], dt[:, h, :],
                           xs[:, h].rearrange("p b t -> p (b t)"), ALU.mult).then_inc(m_dve, 1)
                if R:
                    dve.wait_ge(r_act, at(c[RWKV], R_ACT, "gamma"))
                    wkv_steps(0)
                for l, s in layers(on):
                    gates_1(l)
                if R:
                    wkv_steps(1)
                for l, s in layers(on):
                    gates_2(l)
                if M:
                    scan(0)
                if R:
                    wkv_steps(2)

                for j in range(E):
                    q, h = divmod(j, DH)
                    if R:
                        wkv_steps(j + 3, 0)
                        if j == E - 2:
                            state_and_parts()
                            fraction()
                    if R and j == E - 1 and len(layers(on)) < 2:
                        second_norm()
                    for l, s in layers(on):
                        if R and j == E - 1 and l:
                            second_norm()
                        dve.wait_ge(f_pe[l], at(c[FFN[l]], F_PE[l], f"out{j}"))
                        dve.wait_ge(s_wb[l][j % 2], loads_by(c[s], E // 2, j // 2 + 1))
                        if j:
                            dve.wait_ge(f_pool[l], at(c[FFN[l]], F_POOL[l], f"acc{j - 1}"))
                        stt(out=t1[l][:], in0=OB[l][:], scalar=b2[:, j:j + 1], in1=wb[l][:, j % 2, :],
                            op0=ALU.add, op1=ALU.mult).then_inc(f_dve[l], 1)
                    if M and j + 1 < UNITS:
                        scan(j + 1)
                    if R:
                        wkv_steps(j + 3, 1)
                    if M:
                        dve.wait_ge(m_pool, at(c[MAMBA], M_POOL, f"pairs{j}" if j in PAIRED else f"hc{j}"))
                        if j > DH:
                            dve.wait_ge(m_dve, at(c[MAMBA], M_DVE, f"acc{j - 1}"))
                        dst = (ya[:, h, :] if q == 0 else yr[:]).rearrange("p (b t) -> p b t", b=B)
                        if j in PAIRED:
                            tt(dst, abuf[:, h, 0, :, 1:], abuf[:, h, 1, :, 1:], ALU.add).then_inc(m_dve, 1)
                        else:
                            v.tensor_reduce(dst, abuf[:, h, :, :, 1:].rearrange("p n b t -> p b t n"), AX.X, ALU.add
                                            ).then_inc(m_dve, 1)
                        dve.wait_ge(m_dve, at(c[MAMBA], M_DVE, f"red{j}"))
                        if q:
                            tt(ya[:, h, :], ya[:, h, :], yr[:], ALU.add).then_inc(m_dve, 1)
                if M:
                    dve.wait_ge(m_dve, at(c[MAMBA], M_DVE, f"acc{UNITS - 1}"))
                    for h in range(DH):
                        stt(out=ya[:, h, :], in0=xs[:, h].rearrange("p b t -> p (b t)"), scalar=Dp[:, h:h + 1],
                            in1=ya[:, h, :], op0=ALU.mult, op1=ALU.add).then_inc(m_dve, 1)
                    for h in range(DH):
                        dve.wait_ge(m_dve, at(c[MAMBA], M_DVE, f"y{h}"))
                        dve.wait_ge(m_act, at(c[MAMBA], M_ACT, f"sz{h}"))
                        tt(ya[:, h, :], ya[:, h, :], sz[:, h, :], ALU.mult).then_inc(m_dve, 1)
                if R:
                    dve.wait_ge(r_act, at(c[RWKV], R_ACT, "trc"))
                    dve.wait_ge(r_pe, at(c[RWKV], R_PE, "kv"))
                    stt(out=tr[:], in0=tr[:], scalar=1.0, in1=A1[:], op0=ALU.add, op1=ALU.mult).then_inc(r_dve, 1)
                    dve.wait_ge(r_dve, at(c[RWKV], R_DVE, "s"))
                    stt(out=x0[:], in0=tr[:], scalar=0.5, in1=x0[:], op0=ALU.mult, op1=ALU.add).then_inc(r_dve, 1)
                    dve.wait_ge(r_dve, at(c[RWKV], R_DVE, "x2"))
                    tt(chunk[RWKV], x0[:], xin[:], ALU.add).then_inc(r_dve, 1)
                if M:
                    dve.wait_ge(m_pe, at(c[MAMBA], M_PE, "out"))
                    stt(out=chunk[MAMBA], in0=M0[:], scalar=gate[:], in1=chunk[MAMBA], op0=ALU.mult, op1=ALU.add
                        ).then_inc(m_dve, 1)
                if on == FIRST:
                    finish_weights()
                if R:
                    dve.sem_clear(s_wkv)
                for l, s in layers(on):
                    dve.sem_clear(s_top[l])
                meet(dve, dve_done, i)

            pipeline(dve, iteration)


_INS = ["L0_attn_a_x", "L0_attn_a_time_decay", "L0_attn_a_time_first", "L0_attn_a_time_shift", "L0_attn_a_Wk",
        "L0_attn_a_Wv", "L0_attn_a_Wr", "L0_attn_a_Wck", "L0_attn_a_Wcv", "L0_attn_a_Wcr", "L0_attn_a_ln1_g",
        "L0_attn_a_ln1_b", "L0_attn_a_ln2_g", "L0_attn_a_ln2_b", "L0_attn_b_W_in", "L0_attn_b_A_log",
        "L0_attn_b_W_B", "L0_attn_b_W_C", "L0_attn_b_W_dt", "L0_attn_b_b_dt", "L0_attn_b_D",
        "L0_attn_b_output_gate", "L0_attn_b_W_out", "L0_ffn_rw1", "L0_ffn_rb1", "L0_ffn_rw2", "L0_ffn_rb2",
        "L0_ffn_w1", "L0_ffn_b1", "L0_ffn_w2", "L0_ffn_b2"]
_COLUMNS = ("time_decay", "time_first", "ln1_g", "ln1_b", "ln2_g", "ln2_b")


def kernel(**inputs):
    import numpy as _np
    import concourse.bacc as _bacc
    from concourse import mybir as _mybir
    from concourse.bass_utils import run_bass_kernel_spmd as _run

    nc = _bacc.Bacc("TRN2", target_bir_lowering=False, num_devices=1)
    arrays, aps = {}, {}
    for name in _INS:
        x = _np.ascontiguousarray(inputs[name])
        arrays[f"in_{name}_dram"] = x
        ap = nc.dram_tensor(f"in_{name}_dram", x.shape, _mybir.dt.from_np(x.dtype), kind="ExternalInput").ap()
        short = name.removeprefix("L0_attn_a_").removeprefix("L0_attn_b_").removeprefix("L0_ffn_")
        if short in _COLUMNS:
            ap = ap.unsqueeze(1)
        if short == "time_shift":
            short, ap = "ts", ap.rearrange("a b c -> c (a b)")
        if short == "x":
            ap = ap.rearrange("b (n t) c -> b n t c", t=TC)
        aps[short] = ap
    out = nc.dram_tensor("out_0_dram", (B, T, C), F32, kind="ExternalOutput").ap()
    build(nc, aps, out.rearrange("b (n t) c -> b n t c", t=TC))
    r = _run(nc, [arrays], core_ids=[0])
    return _np.asarray(r.results[0]["out_0_dram"])
```
